# Optimizing a Trainium2 kernel written in Bass

```python
import numpy as np
import jax
import jax.numpy as jnp

def _softmax(x, axis=-1):
    return jax.nn.softmax(x, axis=axis)

def _gelu(x):
    return jax.nn.gelu(x, approximate=True)

def _silu(x):
    return jax.nn.silu(x)

def _sigmoid(x):
    return jax.nn.sigmoid(x)

def _layernorm(x, axis=-1, eps=1e-05):
    m = jnp.mean(x, axis=axis, keepdims=True)
    v = jnp.var(x, axis=axis, keepdims=True)
    return (x - m) / jnp.sqrt(v + eps)

def _scatter_add(tgt, idx, src, axis=0):
    return tgt.at[idx].add(src)

def _segment_sum(src, seg, n):
    return jax.ops.segment_sum(src, seg, n)
kernel_name = 'mk_dlrm_tower_d1_rec_r8_6da897'

def setup_inputs(seed: int=0):
    np.random.seed(seed)
    _w = jnp.asarray

    def _rec_inputs():
        import jax
        import jax.numpy as jnp
        _tk = jax.random.key(seed)
        dense_ctx = jax.random.normal(jax.random.fold_in(_tk, 190), (2048, 16), jnp.float32)
        ids = jnp.stack([jax.random.randint(jax.random.fold_in(_tk, 200 + f), (2048,), 0, v, jnp.int32) for f, v in enumerate([125000, 125000, 1250, 125000, 1000, 1250, 12500, 1000, 1000, 125000, 1250, 1250, 12500, 1000, 12500, 1000, 125000, 125000, 12500, 12500, 125000, 1000, 12500, 12500, 125000, 12500, 12500, 12500, 1250, 12500, 1000, 1250, 12500, 1250, 1000, 12500, 1000, 1000, 125000])], axis=1)
        tbl_0 = 0.05 * jax.random.normal(jax.random.fold_in(_tk, 500 + 0), (125000, 16), jnp.float32)
        tbl_1 = 0.05 * jax.random.normal(jax.random.fold_in(_tk, 500 + 1), (125000, 16), jnp.float32)
        tbl_2 = 0.05 * jax.random.normal(jax.random.fold_in(_tk, 500 + 2), (1250, 16), jnp.float32)
        tbl_3 = 0.05 * jax.random.normal(jax.random.fold_in(_tk, 500 + 3), (125000, 16), jnp.float32)
        tbl_4 = 0.05 * jax.random.normal(jax.random.fold_in(_tk, 500 + 4), (1000, 16), jnp.float32)
        tbl_5 = 0.05 * jax.random.normal(jax.random.fold_in(_tk, 500 + 5), (1250, 16), jnp.float32)
        tbl_6 = 0.05 * jax.random.normal(jax.random.fold_in(_tk, 500 + 6), (12500, 16), jnp.float32)
        tbl_7 = 0.05 * jax.random.normal(jax.random.fold_in(_tk, 500 + 7), (1000, 16), jnp.float32)
        tbl_8 = 0.05 * jax.random.normal(jax.random.fold_in(_tk, 500 + 8), (1000, 16), jnp.float32)
        tbl_9 = 0.05 * jax.random.normal(jax.random.fold_in(_tk, 500 + 9), (125000, 16), jnp.float32)
        tbl_10 = 0.05 * jax.random.normal(jax.random.fold_in(_tk, 500 + 10), (1250, 16), jnp.float32)
        tbl_11 = 0.05 * jax.random.normal(jax.random.fold_in(_tk, 500 + 11), (1250, 16), jnp.float32)
        tbl_12 = 0.05 * jax.random.normal(jax.random.fold_in(_tk, 500 + 12), (12500, 16), jnp.float32)
        tbl_13 = 0.05 * jax.random.normal(jax.random.fold_in(_tk, 500 + 13), (1000, 16), jnp.float32)
        tbl_14 = 0.05 * jax.random.normal(jax.random.fold_in(_tk, 500 + 14), (12500, 16), jnp.float32)
        tbl_15 = 0.05 * jax.random.normal(jax.random.fold_in(_tk, 500 + 15), (1000, 16), jnp.float32)
        tbl_16 = 0.05 * jax.random.normal(jax.random.fold_in(_tk, 500 + 16), (125000, 16), jnp.float32)
        tbl_17 = 0.05 * jax.random.normal(jax.random.fold_in(_tk, 500 + 17), (125000, 16), jnp.float32)
        tbl_18 = 0.05 * jax.random.normal(jax.random.fold_in(_tk, 500 + 18), (12500, 16), jnp.float32)
        tbl_19 = 0.05 * jax.random.normal(jax.random.fold_in(_tk, 500 + 19), (12500, 16), jnp.float32)
        tbl_20 = 0.05 * jax.random.normal(jax.random.fold_in(_tk, 500 + 20), (125000, 16), jnp.float32)
        tbl_21 = 0.05 * jax.random.normal(jax.random.fold_in(_tk, 500 + 21), (1000, 16), jnp.float32)
        tbl_22 = 0.05 * jax.random.normal(jax.random.fold_in(_tk, 500 + 22), (12500, 16), jnp.float32)
        tbl_23 = 0.05 * jax.random.normal(jax.random.fold_in(_tk, 500 + 23), (12500, 16), jnp.float32)
        tbl_24 = 0.05 * jax.random.normal(jax.random.fold_in(_tk, 500 + 24), (125000, 16), jnp.float32)
        tbl_25 = 0.05 * jax.random.normal(jax.random.fold_in(_tk, 500 + 25), (12500, 16), jnp.float32)
        tbl_26 = 0.05 * jax.random.normal(jax.random.fold_in(_tk, 500 + 26), (12500, 16), jnp.float32)
        tbl_27 = 0.05 * jax.random.normal(jax.random.fold_in(_tk, 500 + 27), (12500, 16), jnp.float32)
        tbl_28 = 0.05 * jax.random.normal(jax.random.fold_in(_tk, 500 + 28), (1250, 16), jnp.float32)
        tbl_29 = 0.05 * jax.random.normal(jax.random.fold_in(_tk, 500 + 29), (12500, 16), jnp.float32)
        tbl_30 = 0.05 * jax.random.normal(jax.random.fold_in(_tk, 500 + 30), (1000, 16), jnp.float32)
        tbl_31 = 0.05 * jax.random.normal(jax.random.fold_in(_tk, 500 + 31), (1250, 16), jnp.float32)
        tbl_32 = 0.05 * jax.random.normal(jax.random.fold_in(_tk, 500 + 32), (12500, 16), jnp.float32)
        tbl_33 = 0.05 * jax.random.normal(jax.random.fold_in(_tk, 500 + 33), (1250, 16), jnp.float32)
        tbl_34 = 0.05 * jax.random.normal(jax.random.fold_in(_tk, 500 + 34), (1000, 16), jnp.float32)
        tbl_35 = 0.05 * jax.random.normal(jax.random.fold_in(_tk, 500 + 35), (12500, 16), jnp.float32)
        tbl_36 = 0.05 * jax.random.normal(jax.random.fold_in(_tk, 500 + 36), (1000, 16), jnp.float32)
        tbl_37 = 0.05 * jax.random.normal(jax.random.fold_in(_tk, 500 + 37), (1000, 16), jnp.float32)
        tbl_38 = 0.05 * jax.random.normal(jax.random.fold_in(_tk, 500 + 38), (125000, 16), jnp.float32)
        _rk = jax.random.fold_in(_tk, 7)
        W_top1 = 0.0606339 * jax.random.normal(jax.random.fold_in(_tk, 801), (272, 512), jnp.float32)
        W_top2 = 0.0441942 * jax.random.normal(jax.random.fold_in(_tk, 802), (512, 256), jnp.float32)
        W_top3 = 0.0625 * jax.random.normal(jax.random.fold_in(_tk, 803), (256, 1), jnp.float32)
        b_top1 = jnp.zeros((512,), jnp.float32)
        b_top2 = jnp.zeros((256,), jnp.float32)
        return (dense_ctx, ids, tbl_0, tbl_1, tbl_2, tbl_3, tbl_4, tbl_5, tbl_6, tbl_7, tbl_8, tbl_9, tbl_10, tbl_11, tbl_12, tbl_13, tbl_14, tbl_15, tbl_16, tbl_17, tbl_18, tbl_19, tbl_20, tbl_21, tbl_22, tbl_23, tbl_24, tbl_25, tbl_26, tbl_27, tbl_28, tbl_29, tbl_30, tbl_31, tbl_32, tbl_33, tbl_34, tbl_35, tbl_36, tbl_37, tbl_38, W_top1, b_top1, W_top2, b_top2, W_top3)
    dense_ctx, ids, tbl_0, tbl_1, tbl_2, tbl_3, tbl_4, tbl_5, tbl_6, tbl_7, tbl_8, tbl_9, tbl_10, tbl_11, tbl_12, tbl_13, tbl_14, tbl_15, tbl_16, tbl_17, tbl_18, tbl_19, tbl_20, tbl_21, tbl_22, tbl_23, tbl_24, tbl_25, tbl_26, tbl_27, tbl_28, tbl_29, tbl_30, tbl_31, tbl_32, tbl_33, tbl_34, tbl_35, tbl_36, tbl_37, tbl_38, W_top1, b_top1, W_top2, b_top2, W_top3 = _rec_inputs()

    def _L0_rec_setup():
        import jax, jax.numpy as jnp
        import numpy as np
        B, F0, D = (256, 39, 16)
        LAYER_SIZES = [128, 128, 128]
        key = jax.random.key(seed)
        ks = jax.random.split(key, 1 + 2 * len(LAYER_SIZES))
        inputs = jax.random.normal(ks[0], (B, F0, D), dtype=jnp.float32)
        out = {'inputs': inputs}
        field_nums = [F0]
        for i, size in enumerate(LAYER_SIZES):
            fk = field_nums[-1]
            fan_in = F0 * fk
            scale = np.sqrt(2.0 / (fan_in + size)).astype(np.float32)
            out[f'w{i}'] = jax.random.normal(ks[1 + 2 * i], (F0, fk, size), dtype=jnp.float32) * scale
            out[f'b{i}'] = jnp.zeros((size,), dtype=jnp.float32)
            field_nums.append(size // 2)
        return out
    _L0_rec_all = _L0_rec_setup()
    _L0_rec_in = {k: v for k, v in _L0_rec_all.items() if k in ('w0', 'w1', 'w2', 'b0', 'b1', 'b2')}
    del _L0_rec_all
    return {'dense_ctx': dense_ctx, 'ids': ids, 'tbl_0': tbl_0, 'tbl_1': tbl_1, 'tbl_2': tbl_2, 'tbl_3': tbl_3, 'tbl_4': tbl_4, 'tbl_5': tbl_5, 'tbl_6': tbl_6, 'tbl_7': tbl_7, 'tbl_8': tbl_8, 'tbl_9': tbl_9, 'tbl_10': tbl_10, 'tbl_11': tbl_11, 'tbl_12': tbl_12, 'tbl_13': tbl_13, 'tbl_14': tbl_14, 'tbl_15': tbl_15, 'tbl_16': tbl_16, 'tbl_17': tbl_17, 'tbl_18': tbl_18, 'tbl_19': tbl_19, 'tbl_20': tbl_20, 'tbl_21': tbl_21, 'tbl_22': tbl_22, 'tbl_23': tbl_23, 'tbl_24': tbl_24, 'tbl_25': tbl_25, 'tbl_26': tbl_26, 'tbl_27': tbl_27, 'tbl_28': tbl_28, 'tbl_29': tbl_29, 'tbl_30': tbl_30, 'tbl_31': tbl_31, 'tbl_32': tbl_32, 'tbl_33': tbl_33, 'tbl_34': tbl_34, 'tbl_35': tbl_35, 'tbl_36': tbl_36, 'tbl_37': tbl_37, 'tbl_38': tbl_38, 'W_top1': W_top1, 'b_top1': b_top1, 'W_top2': W_top2, 'b_top2': b_top2, 'W_top3': W_top3, 'L0_rec_w0': _L0_rec_in['w0'], 'L0_rec_w1': _L0_rec_in['w1'], 'L0_rec_w2': _L0_rec_in['w2'], 'L0_rec_b0': _L0_rec_in['b0'], 'L0_rec_b1': _L0_rec_in['b1'], 'L0_rec_b2': _L0_rec_in['b2']}

def reference(dense_ctx, ids, tbl_0, tbl_1, tbl_2, tbl_3, tbl_4, tbl_5, tbl_6, tbl_7, tbl_8, tbl_9, tbl_10, tbl_11, tbl_12, tbl_13, tbl_14, tbl_15, tbl_16, tbl_17, tbl_18, tbl_19, tbl_20, tbl_21, tbl_22, tbl_23, tbl_24, tbl_25, tbl_26, tbl_27, tbl_28, tbl_29, tbl_30, tbl_31, tbl_32, tbl_33, tbl_34, tbl_35, tbl_36, tbl_37, tbl_38, W_top1, b_top1, W_top2, b_top2, W_top3, L0_rec_w0, L0_rec_w1, L0_rec_w2, L0_rec_b0, L0_rec_b1, L0_rec_b2):
    import jax
    import jax.numpy as jnp

    def _L0_rec_ref(inputs, w0, w1, w2, b0, b1, b2):
        import jax, jax.numpy as jnp
        import numpy as np
        B, F0, D = (256, 39, 16)
        LAYER_SIZES = [128, 128, 128]
        x0 = inputs
        xk = inputs
        params = [(w0, b0), (w1, b1), (w2, b2)]
        n_layers = len(params)
        direct = []
        for idx, (W, b) in enumerate(params):
            z = jnp.einsum('bhd,bkd,hks->bsd', x0, xk, W) + b[None, :, None]
            z = jax.nn.relu(z)
            if idx != n_layers - 1:
                half = z.shape[1] // 2
                xk = z[:, :half, :]
                direct.append(z[:, half:, :])
            else:
                direct.append(z)
        logit = jnp.sum(jnp.concatenate(direct, axis=1), axis=-1)
        return logit
    e = jnp.stack([tbl_0[ids[:, 0]], tbl_1[ids[:, 1]], tbl_2[ids[:, 2]], tbl_3[ids[:, 3]], tbl_4[ids[:, 4]], tbl_5[ids[:, 5]], tbl_6[ids[:, 6]], tbl_7[ids[:, 7]], tbl_8[ids[:, 8]], tbl_9[ids[:, 9]], tbl_10[ids[:, 10]], tbl_11[ids[:, 11]], tbl_12[ids[:, 12]], tbl_13[ids[:, 13]], tbl_14[ids[:, 14]], tbl_15[ids[:, 15]], tbl_16[ids[:, 16]], tbl_17[ids[:, 17]], tbl_18[ids[:, 18]], tbl_19[ids[:, 19]], tbl_20[ids[:, 20]], tbl_21[ids[:, 21]], tbl_22[ids[:, 22]], tbl_23[ids[:, 23]], tbl_24[ids[:, 24]], tbl_25[ids[:, 25]], tbl_26[ids[:, 26]], tbl_27[ids[:, 27]], tbl_28[ids[:, 28]], tbl_29[ids[:, 29]], tbl_30[ids[:, 30]], tbl_31[ids[:, 31]], tbl_32[ids[:, 32]], tbl_33[ids[:, 33]], tbl_34[ids[:, 34]], tbl_35[ids[:, 35]], tbl_36[ids[:, 36]], tbl_37[ids[:, 37]], tbl_38[ids[:, 38]]], axis=1)
    z = _L0_rec_ref(e, L0_rec_w0, L0_rec_w1, L0_rec_w2, L0_rec_b0, L0_rec_b1, L0_rec_b2)
    z = z.reshape(z.shape[0], -1)
    h = jnp.concatenate([z, dense_ctx], axis=1)
    h = jnp.maximum(h @ W_top1 + b_top1, 0.0)
    h = jnp.maximum(h @ W_top2 + b_top2, 0.0)
    y = h @ W_top3
    return y

_drawn_inputs = setup_inputs


def setup_inputs(seed=0):
    import zlib

    import numpy as np

    out = dict(_drawn_inputs(seed))
    spreads = {'b_top1': (0.0, 2.0),
     'b_top2': (0.0, 2.0),
     'L0_rec_b0': (0.0, 0.357),
     'L0_rec_b1': (0.0, 0.536),
     'L0_rec_b2': (0.0, 0.8)}
    factors = {'tbl_0': 8.0,
     'tbl_1': 8.0,
     'tbl_2': 8.0,
     'tbl_3': 8.0,
     'tbl_4': 8.0,
     'tbl_5': 8.0,
     'tbl_6': 8.0,
     'tbl_7': 8.0,
     'tbl_8': 8.0,
     'tbl_9': 8.0,
     'tbl_10': 8.0,
     'tbl_11': 8.0,
     'tbl_12': 8.0,
     'tbl_13': 8.0,
     'tbl_14': 8.0,
     'tbl_15': 8.0,
     'tbl_16': 8.0,
     'tbl_17': 8.0,
     'tbl_18': 8.0,
     'tbl_19': 8.0,
     'tbl_20': 8.0,
     'tbl_21': 8.0,
     'tbl_22': 8.0,
     'tbl_23': 8.0,
     'tbl_24': 8.0,
     'tbl_25': 8.0,
     'tbl_26': 8.0,
     'tbl_27': 8.0,
     'tbl_28': 8.0,
     'tbl_29': 8.0,
     'tbl_30': 8.0,
     'tbl_31': 8.0,
     'tbl_32': 8.0,
     'tbl_33': 8.0,
     'tbl_34': 8.0,
     'tbl_35': 8.0,
     'tbl_36': 8.0,
     'tbl_37': 8.0,
     'tbl_38': 8.0,
     'L0_rec_w0': 8.0,
     'L0_rec_w1': 6.246,
     'L0_rec_w2': 4.755,
     'dense_ctx': 8.0}
    for name, (base, spread) in spreads.items():
        noise = np.random.default_rng([zlib.crc32(name.encode()), seed]).standard_normal(out[name].shape)
        drawn = base * np.exp(spread * noise) if base else spread * noise
        out[name] = jnp.asarray(drawn.astype(out[name].dtype))
    for name, factor in factors.items():
        out[name] = (out[name] * factor).astype(out[name].dtype)
    return out
```

```python
from contextlib import ExitStack

import concourse.bass as bass
from concourse import mybir

P = 128
B = 2048
F = 39
D = 16
S = 128
HALF = S // 2
BT = B // P
LANES = 4
Q = D // LANES
CHUNK = LANES * P
CHUNKS = BT * Q
PARTS = 3
ROT = 3
ROWS0 = ROT * F
ROTATIONS = list(range(1, (F + 1) // 2)) + [0]
T0 = -(-len(ROTATIONS) // ROT)
T1 = (F + 1) // 2
I0 = (T0 + 1) // 2
I1 = T1 // 2
SELS = I0 + I1
ITEMS = I0 + 2 * I1
RING = 6
H1 = 512
H2 = 256
DENSE = 16
M1 = H1 // P
M2 = H2 // P
NB = 512
VOCAB = [125000, 125000, 1250, 125000, 1000, 1250, 12500, 1000, 1000, 125000, 1250, 1250, 12500, 1000, 12500,
         1000, 125000, 125000, 12500, 12500, 125000, 1000, 12500, 12500, 125000, 12500, 12500, 12500, 1250,
         12500, 1000, 1250, 12500, 1250, 1000, 12500, 1000, 1000, 125000]

ALU = mybir.AluOpType
ACT = mybir.ActivationFunctionType
F32 = mybir.dt.float32
BF16 = mybir.dt.bfloat16
I32 = mybir.dt.int32

assert I0 % 2 == 0 and I1 % 2 == 0 and ITEMS % RING == 0 and Q % 2 == 0


def wait_past(eng, sem, value):
    if not isinstance(value, int) or value > 0:
        eng.wait_ge(sem, value)


def dlrm_tower(nc, tables, ids, dense_t, sel, ident, w0a, w0b, w1, w2, cin_bias, wt1, bt1, wt2, bt2, wt3, out):
    with ExitStack() as ctx:
        def sb(name, shape, dt=F32):
            return ctx.enter_context(nc.sbuf_tensor(name, shape, dt))

        def ps(name, shape, dt=F32):
            return ctx.enter_context(nc.psum_tensor(name, shape, dt))

        def sem(name):
            return ctx.enter_context(nc.semaphore(name))

        sel_sb = sb("sel_sb", [PARTS * F, 2 * SELS, P], BF16)
        ident_sb = sb("ident_sb", [P, P], BF16)
        w0a_sb = sb("w0a_sb", [P, T0, S])
        w0b_sb = sb("w0b_sb", [P, T0, S])
        w0_sb = sb("w0_sb", [P, T0, S])
        w1_sb = sb("w1_sb", [P, T1, S])
        w2_sb = sb("w2_sb", [P, T1, S])
        cb_sb = sb("cb_sb", [P, 3])
        wt1_sb = sb("wt1_sb", [P, 2, H1])
        wt1d_sb = sb("wt1d_sb", [DENSE, H1])
        dense_sb = sb("dense_sb", [DENSE, B])
        wt2_sb = sb("wt2_sb", [P, M1, H2])
        wt3_sb = sb("wt3_sb", [P, M2])
        bt1_sb = sb("bt1_sb", [P, M1])
        bt2_sb = sb("bt2_sb", [P, M2])
        ids_sb = sb("ids_sb", [P, F], I32)
        emb = sb("emb", [P, F, D])
        rem = sb("rem", [P, F, D])
        rem2 = sb("rem2", [P, F, D])
        parts = sb("parts", [P, D, PARTS * F], BF16)
        x0parts = sb("x0parts", [PARTS * F, CHUNK], BF16)
        x0stack = sb("x0stack", [P, CHUNK])
        x0rep = sb("x0rep", [P, T1, CHUNK])
        maps1 = sb("maps1", [P, CHUNK])
        maps2 = sb("maps2", [P, CHUNK])
        prod = sb("prod", [P, RING, 2, CHUNK])
        direct = sb("direct", [P, 2, 2, CHUNK])
        lanesum = sb("lanesum", [P, 2, CHUNK // 2])
        logit = sb("logit", [P, 2, B])
        y_sb = sb("y_sb", [1, B])

        ps_sel = ps("ps_sel", [P, 2, 2, CHUNK])
        ps_z0 = ps("ps_z0", [P, CHUNK])
        ps_z1 = ps("ps_z1", [P, CHUNK])
        ps_z2 = ps("ps_z2", [P, CHUNK])
        ps_xt = ps("ps_xt", [P, CHUNK], BF16)

        s_cin_w = sem("s_cin_w")
        s_mlp_w = sem("s_mlp_w")
        s_ids = sem("s_ids")
        s_gather = sem("s_gather")
        s_w0 = sem("s_w0")
        s_step = sem("s_step")
        s_split = sem("s_split")
        s_xt = sem("s_xt")
        s_x0 = sem("s_x0")
        s_sel = sem("s_sel")
        s_stack = sem("s_stack")
        s_rep = sem("s_rep")
        s_prod = sem("s_prod")
        s_used = sem("s_used")
        s_relu0 = sem("s_relu0")
        s_relu1 = sem("s_relu1")
        s_relu2 = sem("s_relu2")
        s_add = sem("s_add")
        s_sum = sem("s_sum")
        s_h1 = sem("s_h1")
        s_h1r = sem("s_h1r")
        s_h2 = sem("s_h2")
        s_h2r = sem("s_h2r")
        s_y = sem("s_y")
        s_yc = sem("s_yc")
        s_out = sem("s_out")

        CIN_LOADS = 7
        MLP_LOADS = 7
        ADDS = 2 * Q
        block = ctx.enter_context(nc.Block())

        def base(c):
            return I0 + ITEMS * c

        @block.sync
        def _(sp):
            sp.dma_start(ids_sb[:, :], ids[0]).then_inc(s_ids, 16)
            for dst, src in ((sel_sb[:, :, :], sel), (ident_sb[:, :], ident), (w0a_sb[:, :, :], w0a),
                             (w0b_sb[:, :, :], w0b), (w1_sb[:, :, :], w1), (w2_sb[:, :, :], w2),
                             (cb_sb[:, :], cin_bias)):
                sp.dma_start(dst, src).then_inc(s_cin_w, 16)
            for dst, src in ((wt1_sb[:, :, :], wt1[0:2 * P, :].rearrange("(k p) m -> p k m", p=P)),
                             (wt1d_sb[:, :], wt1[2 * P:, :]), (dense_sb[:, :], dense_t),
                             (wt2_sb[:, :, :], wt2.rearrange("(k p) m -> p k m", p=P)),
                             (wt3_sb[:, :], wt3), (bt1_sb[:, :], bt1), (bt2_sb[:, :], bt2)):
                sp.dma_start(dst, src).then_inc(s_mlp_w, 16)
            with sp.Fori(0, BT - 1) as t:
                sp.wait_ge(s_gather, 16 * F * (t + 1))
                sp.dma_start(ids_sb[:, :], ids[bass.ds(t + 1, 1), :, :].rearrange("o p f -> (o p) f")) \
                    .then_inc(s_ids, 16)
            sp.wait_ge(s_yc, B // NB)
            sp.dma_start(out.rearrange("b o -> o b"), y_sb[:, :]).then_inc(s_out, 16)
            sp.wait_ge(s_out, 16)

        @block.gpsimd
        def _(pool):
            def gather(t):
                pool.wait_ge(s_ids, 16 * (t + 1))
                pool.nop(nofuse=True)
                for f in range(F):
                    pool.indirect_dma_start(
                        emb[:, f, :], None, tables[f][:, :],
                        bass.IndirectOffsetOnAxis(ap=ids_sb[:, f:f + 1], axis=0)).then_inc(s_gather, 16)

            def lane_sums(t, q):
                c, half = Q * t + q, CHUNK // 2
                r = direct[:, q % 2, :, :]
                pool.wait_ge(s_relu0, 3 * (c + 1))
                pool.wait_ge(s_relu1, 3 * (c + 1))
                pool.wait_ge(s_relu2, c + 1)
                done = ADDS * t + (2 * q - 1 if q else 0)
                wait_past(pool, s_add, done)
                if q == 0:
                    pool.tensor_tensor(lanesum[:, :, :], r[:, :, 0:half], r[:, :, half:], ALU.add) \
                        .then_inc(s_add, 1)
                    pool.wait_ge(s_add, done + 1)
                else:
                    pool.tensor_tensor(lanesum[:, :, :], lanesum[:, :, :], r[:, :, 0:half], ALU.add) \
                        .then_inc(s_add, 1)
                    pool.wait_ge(s_add, done + 1)
                    pool.tensor_tensor(lanesum[:, :, :], lanesum[:, :, :], r[:, :, half:], ALU.add) \
                        .then_inc(s_add, 1)
                    pool.wait_ge(s_add, done + 2)
                pool.sem_inc(s_sum, 1)
                if q == Q - 1:
                    pool.tensor_tensor(logit[:, :, bass.ds(P * t, P)], lanesum[:, :, 0:P], lanesum[:, :, P:half],
                                       ALU.add).then_inc(s_add, 1)

            gather(0)
            def tile(t):
                pool.wait_ge(s_split, t + 1)
                gather(t + 1)
                for q in range(Q):
                    lane_sums(t, q)

            tile(0)
            with pool.Fori(1, BT - 1) as t:
                tile(t)
            for q in range(Q):
                lane_sums(BT - 1, q)

        @block.vector
        def _(dve):
            def split(t):
                dve.wait_ge(s_gather, 16 * F * (t + 1))
                steps = ((emb, None), (rem, emb), (rem2, rem))
                for i, (src, before) in enumerate(steps):
                    if i:
                        dve.wait_ge(s_step, 5 * t + 2 * i - 1)
                        nc.vector.tensor_tensor(
                            src[:, :, :], before[:, :, :],
                            parts[:, :, F * (i - 1):F * i].rearrange("p d f -> p f d"),
                            ALU.subtract).then_inc(s_step, 1)
                        dve.wait_ge(s_step, 5 * t + 2 * i)
                    last = nc.vector.tensor_copy(parts[:, :, F * i:F * (i + 1)].rearrange("p d f -> p f d"),
                                                 src[:, :, :])
                    last.then_inc(s_step, 1)
                dve.wait_ge(s_step, 5 * t + 5)
                nc.vector.sem_inc(s_split, 1)

            def product(item, slot, tiles, in0, in1):
                wait_past(dve, s_used, item + 1 - RING)
                nc.vector.tensor_tensor(prod[:, slot, 0:tiles, :], in0, in1, ALU.mult).then_inc(s_prod, 1)

            def twice(x):
                return x[:, None, :].broadcast_to([P, 2, CHUNK])

            def layer0(n, first, slot):
                dve.wait_ge(s_stack, n + 1)
                for k in range(I0):
                    dve.wait_ge(s_sel, SELS * n + k + 1)
                    if k == 0:
                        args = (1, x0stack[:, None, :], ps_sel[:, 0, 1:2, :])
                    else:
                        args = (2, twice(x0stack), ps_sel[:, k % 2, :, :])
                    product(first + k, (slot + k) % RING, *args)

            def wide(c, first, off, maps, ready, value):
                dve.wait_ge(ready, value)
                for j in range(I1):
                    dve.wait_ge(s_rep, I1 * c + j + 1)
                    product(first + j, (I0 + off + j) % RING, 2, x0rep[:, 2 * j:2 * j + 2, :], twice(maps))

            def step(t, q, last=False):
                c = Q * t + q
                wide(c, base(c), 0, maps1, s_relu0, 3 * c + 2)
                if q == Q - 2 and not last:
                    dve.wait_ge(s_xt, c + 2)
                    split(t + 1)
                if not (last and q == Q - 1):
                    layer0(c + 1, base(c) + I1, I0 + I1)
                off = I1 if last and q == Q - 1 else I1 + I0
                wide(c, base(c) + off, off, maps2, s_relu1, 3 * c + 2)

            split(0)
            dve.wait_ge(s_cin_w, 16 * CIN_LOADS)
            nc.vector.tensor_tensor(w0_sb[:, :, :], w0a_sb[:, :, :], w0b_sb[:, :, :], ALU.add).then_inc(s_w0, 1)
            layer0(0, 0, 0)
            for q in range(Q):
                step(0, q)
            with dve.Fori(1, BT - 1) as t:
                for q in range(Q):
                    step(t, q)
            for q in range(Q):
                step(BT - 1, q, last=True)

        @block.scalar
        def _(act):
            def x0_copy(n):
                act.wait_ge(s_xt, n + 1)
                wait_past(act, s_sel, SELS * n)
                nc.scalar.activation(x0parts[:, :], ps_xt[0:PARTS * F, :], ACT.Copy).then_inc(s_x0, 1)

            def stack_copy(n, made):
                act.wait_ge(s_sel, SELS * n + 1)
                wait_past(act, s_prod, made)
                nc.scalar.activation(x0stack[:, :], ps_sel[:, 0, 0, :], ACT.Copy).then_inc(s_stack, 1)

            def relu(z, layer, lo, maps, dest, done):
                other = HALF - lo
                for at in (0, HALF):
                    nc.scalar.activation(maps[at:at + HALF, :], z[lo:lo + HALF, :], ACT.Relu,
                                         bias=cb_sb[lo:lo + HALF, layer:layer + 1]).then_inc(done, 1)
                nc.scalar.activation(dest[other:other + HALF, :], z[other:other + HALF, :], ACT.Relu,
                                     bias=cb_sb[other:other + HALF, layer:layer + 1]).then_inc(done, 1)

            def relu0(n, parity, contracted, summed):
                act.wait_ge(s_used, contracted)
                wait_past(act, s_sum, summed)
                relu(ps_z0, 0, 0, maps1, direct[:, parity, 0, :], s_relu0)

            def rep_copy(n, j, made):
                act.wait_ge(s_sel, SELS * n + I0 + j + 1)
                wait_past(act, s_prod, made)
                nc.scalar.activation(x0rep[:, 2 * j:2 * j + 2, :], ps_sel[:, j % 2, :, :], ACT.Copy) \
                    .then_inc(s_rep, 1)

            def step(t, q, last=False):
                c = Q * t + q
                more = not (last and q == Q - 1)
                skip = 0 if more else I0
                if more:
                    x0_copy(c + 1)
                    stack_copy(c + 1, base(c))
                act.wait_ge(s_used, base(c) + I1)
                relu(ps_z1, 1, HALF, maps2, direct[:, q % 2, 0, :], s_relu1)
                if more:
                    relu0(c + 1, (q + 1) % 2, base(c) + I1 + I0, c)
                    for j in range(I1):
                        rep_copy(c + 1, j, base(c) + I1 + I0 + j + 1)
                act.wait_ge(s_used, base(c) + ITEMS - skip)
                nc.scalar.activation(direct[:, q % 2, 1, :], ps_z2[:, :], ACT.Relu,
                                     bias=cb_sb[:, 2:3]).then_inc(s_relu2, 1)

            act.wait_ge(s_cin_w, 16 * CIN_LOADS)
            x0_copy(0)
            stack_copy(0, 0)
            relu0(0, 0, I0, 0)
            for j in range(I1):
                rep_copy(0, j, 0)
            for q in range(Q):
                step(0, q)
            with act.Fori(1, BT - 1) as t:
                for q in range(Q):
                    step(t, q)
            for q in range(Q):
                step(BT - 1, q, last=True)

            act.wait_ge(s_mlp_w, 16 * MLP_LOADS)
            def mlp(n):
                for m in range(M1):
                    act.wait_ge(s_h1, M1 * n + m + 1)
                    if m == 0:
                        wait_past(act, s_h2, M2 * n)
                    nc.scalar.activation(x0rep[:, m, :], ps_sel[:, m // 2, m % 2, :], ACT.Relu,
                                         bias=bt1_sb[:, m:m + 1]).then_inc(s_h1r, 1)
                for m, z in enumerate((ps_z0, ps_z1)):
                    act.wait_ge(s_h2, M2 * n + m + 1)
                    if m == 0:
                        wait_past(act, s_y, n)
                    nc.scalar.activation(x0rep[:, M1 + m, :], z[:, :], ACT.Relu,
                                         bias=bt2_sb[:, m:m + 1]).then_inc(s_h2r, 1)
                act.wait_ge(s_y, n + 1)
                nc.scalar.activation(y_sb[0:1, bass.ds(NB * n, NB)], ps_z2[0:1, :], ACT.Copy).then_inc(s_yc, 1)

            mlp(0)
            with act.Fori(1, B // NB) as n:
                mlp(n)

        @block.tensor
        def _(pe):
            def transposes(n, q):
                wait_past(pe, s_x0, n)
                for d in range(LANES):
                    last = nc.tensor.transpose(ps_xt[0:PARTS * F, P * d:P * (d + 1)],
                                               parts[:, LANES * q + d, :], ident_sb[:, :])
                last.then_inc(s_xt, 1)

            def select(g):
                for i in range(2):
                    last = nc.tensor.matmul(ps_sel[:, g % 2, i, :], sel_sb[:, 2 * g + i, :], x0parts[:, :],
                                            start=True, stop=True)
                last.then_inc(s_sel, 1)

            def select0(n, k, made):
                if k == 0:
                    pe.wait_ge(s_x0, n + 1)
                if k < 2:
                    wait_past(pe, s_rep, I1 * n - 1 + k)
                else:
                    pe.wait_ge(s_stack, n + 1)
                    pe.wait_ge(s_prod, made)
                select(k)

            def select_rep(n, j, made):
                if j < 2:
                    pe.wait_ge(s_prod, made)
                else:
                    pe.wait_ge(s_rep, I1 * n + j - 1)
                select(I0 + j)

            def contract(item, slot, w, tiles, z, first, final):
                pe.wait_ge(s_prod, item + 1)
                for i, tile in enumerate(tiles):
                    last = nc.tensor.matmul(z[:, :], w[:, tile, :], prod[:, slot, i, :],
                                            start=first and i == 0, stop=final and i == len(tiles) - 1)
                last.then_inc(s_used, 1)

            def layer0(n, item, slot):
                wait_past(pe, s_relu0, 3 * n)
                for k in range(I0):
                    tiles = (0,) if k == 0 else (2 * k - 1, 2 * k)
                    contract(item + k, (slot + k) % RING, w0_sb, tiles, ps_z0, k == 0, k == I0 - 1)

            def step(t, q, last=False):
                c = Q * t + q
                n = c + 1
                more = not (last and q == Q - 1)
                b = base(c)
                if more:
                    if q == Q - 1:
                        pe.wait_ge(s_split, t + 2)
                    transposes(n, (q + 1) % Q)
                wait_past(pe, s_relu1, 3 * c)
                before = {3: 0, 4: 1, 8: 2, 9: 3}
                for j in range(I1):
                    if more and j in before:
                        k = before[j]
                        select0(n, k, b + I1 + k - 1)
                    contract(b + j, (I0 + j) % RING, w1_sb, (2 * j, 2 * j + 1), ps_z1, j == 0, j == I1 - 1)
                if more:
                    layer0(n, b + I1, I0 + I1)
                    b = b + I0
                wait_past(pe, s_relu2, c)
                for j in range(I1):
                    if more:
                        select_rep(n, j, b + I1 - 1 + j)
                    slot = (I0 + I1 + (I0 if more else 0) + j) % RING
                    contract(b + I1 + j, slot, w2_sb, (2 * j, 2 * j + 1), ps_z2, j == 0, j == I1 - 1)

            pe.wait_ge(s_cin_w, 16 * CIN_LOADS)
            pe.wait_ge(s_split, 1)
            transposes(0, 0)
            for k in range(I0):
                select0(0, k, k - 1)
            pe.wait_ge(s_w0, 1)
            layer0(0, 0, 0)
            for j in range(I1):
                select_rep(0, j, I0 - 1 + j)
            for q in range(Q):
                step(0, q)
            with pe.Fori(1, BT - 1) as t:
                for q in range(Q):
                    step(t, q)
            for q in range(Q):
                step(BT - 1, q, last=True)

            pe.wait_ge(s_mlp_w, 16 * MLP_LOADS)
            pe.wait_ge(s_add, ADDS * BT)
            pe.wait_ge(s_relu2, CHUNKS)
            def mlp(n):
                cols = bass.ds(NB * n, NB)
                for m in range(M1):
                    wait_past(pe, s_h1r, M1 * n)
                    z, ms = ps_sel[:, m // 2, m % 2, :], slice(P * m, P * (m + 1))
                    for k in range(2):
                        nc.tensor.matmul(z, wt1_sb[:, k, ms], logit[:, k, cols], start=k == 0, stop=False)
                    nc.tensor.matmul(z, wt1d_sb[:, ms], dense_sb[:, cols], start=False, stop=True) \
                        .then_inc(s_h1, 1)
                wait_past(pe, s_h2r, M2 * n)
                for m, z in enumerate((ps_z0, ps_z1)):
                    for k in range(M1):
                        pe.wait_ge(s_h1r, M1 * n + k + 1)
                        last = nc.tensor.matmul(z[:, :], wt2_sb[:, k, P * m:P * (m + 1)], x0rep[:, k, :],
                                                start=k == 0, stop=k == M1 - 1)
                    last.then_inc(s_h2, 1)
                wait_past(pe, s_yc, n)
                for k in range(M2):
                    pe.wait_ge(s_h2r, M2 * n + k + 1)
                    last = nc.tensor.matmul(ps_z2[0:1, :], wt3_sb[:, k:k + 1], x0rep[:, M1 + k, :],
                                            start=k == 0, stop=k == M2 - 1)
                last.then_inc(s_y, 1)

            mlp(0)
            with pe.Fori(1, B // NB) as n:
                mlp(n)


def kernel(**inputs):
    import ml_dtypes
    import numpy as np
    import concourse.bacc as bacc
    from concourse.bass_utils import run_bass_kernel_spmd as run

    f32 = np.float32
    x = {k: np.asarray(v) for k, v in inputs.items()}

    w0 = x["L0_rec_w0"]
    w0a, w0b = np.zeros((P, T0, S), f32), np.zeros((P, T0, S), f32)
    sel = np.zeros((PARTS * F, 2 * SELS, P), ml_dtypes.bfloat16)
    h = np.arange(F)
    rows = [part * F for part in range(PARTS)]
    for i in range(ROT):
        for r0 in rows:
            sel[r0 + h, 0, i * F + h] = 1
    for n, r in enumerate(ROTATIONS):
        t, i = divmod(n, ROT)
        k = (h + r) % F
        w0a[i * F + h, t] = w0[h, k]
        if r:
            w0b[i * F + h, t] = w0[k, h]
        for r0 in rows:
            sel[r0 + k, 1 + t, i * F + h] = 1
    for hh in range(F):
        j, i = divmod(hh, 2)
        for r0 in rows:
            sel[r0 + hh, 2 * I0 + j, i * HALF:(i + 1) * HALF] = 1

    def pairs(w):
        full = np.zeros((2 * T1, HALF, S), f32)
        full[:F] = w
        return np.ascontiguousarray(full.reshape(T1, P, S).transpose(1, 0, 2))

    swap = np.r_[HALF:S, 0:HALF]
    cin_bias = np.stack([x["L0_rec_b0"], x["L0_rec_b1"][swap], x["L0_rec_b2"]], axis=1)
    wt1 = x["W_top1"][np.r_[swap, S:S + S + DENSE]]
    arrays = {
        "ids": np.ascontiguousarray(x["ids"].reshape(BT, P, F)),
        "dense_t": np.ascontiguousarray(x["dense_ctx"].T),
        "sel": sel,
        "ident": np.eye(P, dtype=ml_dtypes.bfloat16),
        "w0a": w0a,
        "w0b": w0b,
        "w1": pairs(x["L0_rec_w1"][:, :, swap]),
        "w2": pairs(x["L0_rec_w2"]),
        "cin_bias": np.ascontiguousarray(cin_bias),
        "wt1": np.ascontiguousarray(wt1),
        "bt1": np.ascontiguousarray(x["b_top1"].reshape(M1, P).T),
        "wt2": x["W_top2"],
        "bt2": np.ascontiguousarray(x["b_top2"].reshape(M2, P).T),
        "wt3": np.ascontiguousarray(x["W_top3"].reshape(M2, P).T),
    }
    tables = {f"tbl_{f}": x[f"tbl_{f}"] for f in range(F)}

    nc = bacc.Bacc("TRN2", target_bir_lowering=False, num_devices=1)

    def dram(name, a):
        return nc.dram_tensor(name, a.shape, mybir.dt.from_np(a.dtype), kind="ExternalInput").ap()

    tbl_aps = [dram(f"tbl_{f}", tables[f"tbl_{f}"]) for f in range(F)]
    aps = {name: dram(name, a) for name, a in arrays.items()}
    out = nc.dram_tensor("out", (B, 1), F32, kind="ExternalOutput").ap()
    dlrm_tower(nc, tbl_aps, out=out, **aps)
    arrays.update(tables)
    r = run(nc, [arrays], core_ids=[0])
    return r.results[0]["out"]
```

```python
from contextlib import ExitStack

import concourse.bass as bass
from concourse import mybir

P = 128
B = 2048
F = 39
D = 16
S = 128
HALF = S // 2
BT = B // P
LANES = 4
Q = D // LANES
CHUNK = LANES * P
CHUNKS = BT * Q
PARTS = 3
ROT = 3
ROWS0 = ROT * F
ROTATIONS = list(range(1, (F + 1) // 2)) + [0]
T0 = -(-len(ROTATIONS) // ROT)
T1 = (F + 1) // 2
I0 = (T0 + 1) // 2
TILES0 = [tuple(range(2 * j, min(2 * j + 2, T0))) for j in range(I0)]
I1 = T1 // 2
PRODS = 8
HIS = 6
LOS = 5
X0_PLACE = 4
SPLIT_PLACE = 5
STACK_PLACE = 7
SELECT_STACK_PLACE = 3
SELECT_AHEAD = 6
GATHER_PLACE = 4
SUM_PLACE = 7
LAG = 3
H1 = 512
H2 = 256
DENSE = 16
M1 = H1 // P
M2 = H2 // P
NB = 512
VOCAB = [125000, 125000, 1250, 125000, 1000, 1250, 12500, 1000, 1000, 125000, 1250, 1250, 12500, 1000, 12500,
         1000, 125000, 125000, 12500, 12500, 125000, 1000, 12500, 12500, 125000, 12500, 12500, 12500, 1250,
         12500, 1000, 1250, 12500, 1250, 1000, 12500, 1000, 1000, 125000]

ALU = mybir.AluOpType
ACT = mybir.ActivationFunctionType
F32 = mybir.dt.float32
BF16 = mybir.dt.bfloat16
I32 = mybir.dt.int32

F32R = mybir.dt.float32r

WHOLE, V, G = "whole", "V", "G"
KINDS1 = [G, V, WHOLE, G, V, G, WHOLE, V, G, WHOLE]
KINDS2 = [WHOLE, G, V, G, WHOLE, V, G, G, V, G]
HEAD2 = 7
LAYER1 = [(1, j, kind) for j, kind in enumerate(KINDS1)]
LAYER0 = [(0, j, WHOLE) for j in range(I0)]
LAYER2 = [(2, j, kind) for j, kind in enumerate(KINDS2)]
HEAD, TAIL = LAYER2[:HEAD2], LAYER2[HEAD2:]
MIDDLE = [TAIL[0], LAYER0[0], TAIL[1], LAYER0[1], TAIL[2], LAYER0[2], LAYER0[3]]
ITEMS = LAYER1 + MIDDLE + HEAD
FIRST_ITEMS = LAYER1 + LAYER0 + HEAD
LAST_ITEMS = LAYER1 + TAIL + HEAD + TAIL
TWICE = len(TAIL)


def count(items, kinds):
    return sum(kind in kinds for _, _, kind in items)


NI = len(ITEMS)
NS = count(ITEMS, (V, G))
WHOLE1, WHOLE2 = ([j for _, j, kind in layer if kind == WHOLE] for layer in (LAYER1, LAYER2))
SPLIT1, SPLIT2 = ([j for _, j, kind in layer if kind != WHOLE] for layer in (LAYER1, LAYER2))
ALL = (WHOLE, V, G)

assert Q % 2 == 0 and NI % PRODS == 0 and NS * Q % HIS == 0 and NS * Q % LOS == 0 and len(TAIL) == 3


def wait_past(eng, sem, value):
    if not isinstance(value, int) or value > 0:
        eng.wait_ge(sem, value)


def before(c, kinds=ALL):
    start = count(LAYER0, kinds)
    if isinstance(c, int) and c == 0:
        return start
    return start + count(FIRST_ITEMS, kinds) + count(ITEMS, kinds) * (c - 1)


def items_of(c):
    if isinstance(c, int):
        return LAYER0 if c < 0 else FIRST_ITEMS if c == 0 else LAST_ITEMS if c == CHUNKS - 1 else ITEMS
    return ITEMS


def upto(c, k, kinds=ALL):
    own = count(items_of(c)[:k + 1], kinds)
    return own if isinstance(c, int) and c < 0 else before(c, kinds) + own


def at(c, layer, j, late=False):
    where = [k for k, item in enumerate(items_of(c)) if item[:2] == (layer, j)]
    return where[-1 if late else 0]


def back(c, k, n, kinds=ALL):
    while True:
        for i in range(k - 1, -1, -1):
            n -= items_of(c)[i][2] in kinds
            if n == 0:
                return c, i
        if isinstance(c, int) and c < 0:
            return None
        c, k = c - 1, len(items_of(c - 1))


def dlrm_tower(nc, tables, ids, dense_t, sel, ident, w0a, w0b, w1_whole, w2_whole, w_split, cin_bias, wt1, bt1, wt2, bt2, wt3,
               x0rows, out):
    with ExitStack() as ctx:
        def sb(name, shape, dt=F32):
            return ctx.enter_context(nc.sbuf_tensor(name, shape, dt))

        def ps(name, shape, dt=F32):
            return ctx.enter_context(nc.psum_tensor(name, shape, dt))

        def sem(name):
            return ctx.enter_context(nc.semaphore(name))

        sel_buf = sb("sel_buf", [P, (T0 + 1) // 2 * P])
        ident_sb = sb("ident_sb", [P, P], BF16)
        w0_sb = sb("w0_sb", [P, T0, S])
        w1_sb = sb("w1_sb", [P, 2 * len(WHOLE1), S])
        w2_sb = sb("w2_sb", [P, 2 * len(WHOLE2), S])
        w_hi = sb("w_hi", [P, NS, 2, S], F32R)
        w_lo = sb("w_lo", [P, NS, 2, S], F32R)
        cb_sb = sb("cb_sb", [P, 3])
        wt3_sb = sb("wt3_sb", [P, M2])
        bt1_sb = sb("bt1_sb", [P, M1])
        bt2_sb = sb("bt2_sb", [P, M2])
        ids_sb = sb("ids_sb", [P, F], I32)
        emb = sb("emb", [P, F, D])
        parts = sb("parts", [P, D, PARTS * F], BF16)
        x0parts = sb("x0parts", [PARTS * F, CHUNK], BF16)
        x0stack = sb("x0stack", [P, CHUNK])
        x0rep = sb("x0rep", [P, TWICE + I1, 2, CHUNK])
        prod = sb("prod", [P, PRODS, 2, CHUNK])
        hi = sb("hi", [P, HIS, 2, CHUNK], F32R)
        lo = sb("lo", [P, LOS, 2, CHUNK], F32R)
        direct = sb("direct", [P, 2, 2, CHUNK])
        lanesum = sb("lanesum", [P, 2, CHUNK // 2])
        logit = sb("logit", [P, 2, B])

        ps_sel = ps("ps_sel", [P, 2, CHUNK])
        maps1 = ps("maps1", [P, CHUNK])
        maps2 = ps("maps2", [P, CHUNK])
        ps_z0 = ps("ps_z0", [P, CHUNK])
        ps_z1 = ps("ps_z1", [P, CHUNK])
        ps_z2 = ps("ps_z2", [P, CHUNK])
        ps_x = ps("ps_x", [P, CHUNK])

        sel_sb = sel_buf[0:PARTS * F, :].bitcast(BF16).rearrange("p (g m) -> p g m", m=P)
        stage0 = prod[:, 0:2, :, :].rearrange("p a b n -> p (a b n)")[:, 0:2 * T0 * S] \
            .rearrange("p (a g m) -> p a g m", a=2, m=S)
        stage = x0rep[:, 0:5, :, :].rearrange("p a b n -> p (a b n)")[:, 0:NS * 2 * S] \
            .rearrange("p (k g m) -> p k g m", g=2, m=S)
        once = x0rep[:, I1 - TWICE:I1, :, :].rearrange("p a b n -> p (a b n)")
        dense_sb = once[0:DENSE, 0:B]
        wt1_sb = once[:, B:B + 2 * H1].rearrange("p (k m) -> p k m", k=2)
        wt2_sb = prod[:, 0, :, :].rearrange("p a n -> p (a n)").rearrange("p (k m) -> p k m", k=M1)
        wt1d_sb = sel_buf[0:DENSE, 0:H1]
        hidden = x0rep[:, 0:3, :, :].rearrange("p a b n -> p (a b) n")
        y_sb = direct[0:1, :, :, :].rearrange("p a b n -> p (a b n)")
        ps_xt = ps_x[:, 0:CHUNK // 2].bitcast(BF16)
        ps_h1 = (ps_sel[:, 0, :], ps_sel[:, 1, :], maps1[:, :], maps2[:, :])

        s_ids = sem("s_ids")
        s_cin_w = sem("s_cin_w")
        s_mlp_c = sem("s_mlp_c")
        s_mlp_w = sem("s_mlp_w")
        s_wt2 = sem("s_wt2")
        s_store = sem("s_store")
        s_rep = [sem(f"s_rep{j}") for j in range(I1)]
        s_gather = sem("s_gather")
        s_w0 = sem("s_w0")
        s_whi = sem("s_whi")
        s_wlo = sem("s_wlo")
        s_step = sem("s_step")
        s_split = sem("s_split")
        s_xt = sem("s_xt")
        s_x0 = sem("s_x0")
        s_sela = sem("s_sela")
        s_sel = sem("s_sel")
        s_stack = sem("s_stack")
        s_prod = sem("s_prod")
        s_hi = sem("s_hi")
        s_lov = sem("s_lov")
        s_log = sem("s_log")
        s_used = sem("s_used")
        s_maps1 = sem("s_maps1")
        s_maps2 = sem("s_maps2")
        s_direct0 = sem("s_direct0")
        s_direct1 = sem("s_direct1")
        s_direct2 = sem("s_direct2")
        s_add = sem("s_add")
        s_sum = sem("s_sum")
        s_h1 = sem("s_h1")
        s_h1r = sem("s_h1r")
        s_h2 = sem("s_h2")
        s_h2r = sem("s_h2r")
        s_y = sem("s_y")
        s_yc = sem("s_yc")
        s_out = sem("s_out")

        CIN_LOADS = 8
        ADDS = 2 * Q
        block = ctx.enter_context(nc.Block())

        def pair(parity, j):
            return x0rep[:, j + (TWICE if parity and j >= HEAD2 else 0), :, :]

        def wait_lo(eng, c, k):
            kind = items_of(c)[k][2]
            eng.wait_ge(s_lov if kind == V else s_log, upto(c, k, (kind,)))

        def wait_split_free(eng, c, k, buffers):
            past = back(c, k, buffers, (V, G))
            if past:
                eng.wait_ge(s_used, upto(*past))

        def prod_slot(c, k):
            if isinstance(c, int) and c < 0:
                return k
            return (before(0 if isinstance(c, int) and c == 0 else 1) + k) % PRODS

        def split_slot(q, c, k, buffers):
            own = count(items_of(c)[:k], (V, G))
            return (before(c if isinstance(c, int) and c == 0 else Q + q, (V, G)) + own) % buffers

        def make_lo(eng, op, c, q, k, done):
            eng.wait_ge(s_hi, upto(c, k, (V, G)))
            wait_split_free(eng, c, k, LOS)
            op(lo[:, split_slot(q, c, k, LOS), :, :], prod[:, prod_slot(c, k), :, :],
               hi[:, split_slot(q, c, k, HIS), :, :].bitcast(F32),
               ALU.subtract).then_inc(done, 1)

        @block.sync
        def _(sp):
            def replicate(n, parity):
                c = n - 1
                sp.wait_ge(s_stack, n + 1)
                sp.nop(nofuse=True)
                if not isinstance(n, int) or n > 1:
                    sp.wait_ge(s_prod, before(c))
                    sp.nop(nofuse=True)
                sp.dma_start(x0rows[parity], x0stack[0:2 * T1, :]).then_inc(s_store, 16)
                sp.wait_ge(s_store, 16 * (n + 1))
                sp.nop(nofuse=True)
                for j in list(range(HEAD2, I1)) + list(range(HEAD2)):
                    if (not isinstance(n, int) or n > 0) and (2, j) in [x[:2] for x in items_of(c)]:
                        sp.wait_ge(s_prod, upto(c, at(c, 2, j)))
                        sp.nop(nofuse=True)
                    for i in range(2):
                        rows = x0rows[parity, 4 * j + i:4 * j + i + 3:2, :]
                        sp.dma_start(pair(parity, j)[HALF * i:HALF * (i + 1), :, :],
                                     rows[None, :, :].broadcast_to([HALF, 2, CHUNK])).then_inc(s_rep[j], 16)

            def load_ids(t):
                sp.wait_ge(s_gather, 16 * F * t)
                sp.nop(nofuse=True)
                sp.dma_start(ids_sb[:, :], ids[bass.ds(t, 1), :, :].rearrange("o p f -> (o p) f")) \
                    .then_inc(s_ids, 16)

            def step(t, q):
                replicate(Q * t + q + 1, (q + 1) % 2)

            sp.dma_start(ids_sb[:, :], ids[0]).then_inc(s_ids, 16)
            for dst, src in ((stage, w_split.rearrange("p (k g) m -> p k g m", g=2)),
                             (stage0[:, 0, :, :], w0a), (stage0[:, 1, :, :], w0b),
                             (sel_sb, sel), (ident_sb[:, :], ident), (w1_sb[:, :, :], w1_whole),
                             (w2_sb[:, :, :], w2_whole), (cb_sb[:, :], cin_bias)):
                sp.dma_start(dst, src).then_inc(s_cin_w, 16)
            for dst, src in ((wt3_sb[:, :], wt3), (bt1_sb[:, :], bt1), (bt2_sb[:, :], bt2)):
                sp.dma_start(dst, src).then_inc(s_mlp_c, 16)
            load_ids(1)
            sp.wait_ge(s_wlo, 1)
            replicate(0, 0)
            step(0, 0)
            step(0, 1)
            with sp.Fori(0, BT - 2) as t:
                load_ids(t + 2)
                for q in range(2, Q):
                    step(t, q)
                for q in range(2):
                    step(t + 1, q)
            for q in range(2, Q):
                step(BT - 2, q)
            for q in range(Q - 1):
                step(BT - 1, q)

            end = CHUNKS - 1
            sp.wait_ge(s_prod, upto(end, at(end, 2, I1 - 1)))
            sp.dma_start(dense_sb, dense_t).then_inc(s_mlp_w, 16)
            sp.dma_start(wt1_sb, wt1[0:2 * P, :].rearrange("(k p) m -> p k m", p=P)).then_inc(s_mlp_w, 16)
            sp.wait_ge(s_sel, I0 * CHUNKS)
            sp.dma_start(wt1d_sb, wt1[2 * P:, :]).then_inc(s_mlp_w, 16)
            sp.wait_ge(s_used, upto(end, len(LAST_ITEMS) - 1))
            sp.dma_start(wt2_sb, wt2.rearrange("(k p) m -> p k m", p=P)).then_inc(s_wt2, 16)
            sp.wait_ge(s_yc, B // NB)
            sp.dma_start(out.rearrange("b o -> o b"), y_sb).then_inc(s_out, 16)
            sp.wait_ge(s_out, 16)

        @block.gpsimd
        def _(pool):
            def gather(t, fields):
                for f in fields:
                    pool.indirect_dma_start(
                        emb[:, f, :], None, tables[f][:, :],
                        bass.IndirectOffsetOnAxis(ap=ids_sb[:, f:f + 1], axis=0)).then_inc(s_gather, 16)

            def lane_sums(t, q):
                c, half = Q * t + q, CHUNK // 2
                r = direct[:, q % 2, :, :]
                pool.wait_ge(s_direct0, c + 1)
                pool.wait_ge(s_direct1, c + 1)
                pool.wait_ge(s_direct2, c + 1)
                done = ADDS * t + (2 * q - 1 if q else 0)
                wait_past(pool, s_add, done)
                if q == 0:
                    pool.tensor_tensor(lanesum[:, :, :], r[:, :, 0:half], r[:, :, half:], ALU.add) \
                        .then_inc(s_add, 1)
                    pool.wait_ge(s_add, done + 1)
                else:
                    pool.tensor_tensor(lanesum[:, :, :], lanesum[:, :, :], r[:, :, 0:half], ALU.add) \
                        .then_inc(s_add, 1)
                    pool.wait_ge(s_add, done + 1)
                    pool.tensor_tensor(lanesum[:, :, :], lanesum[:, :, :], r[:, :, half:], ALU.add) \
                        .then_inc(s_add, 1)
                    pool.wait_ge(s_add, done + 2)
                pool.sem_inc(s_sum, 1)
                if q == Q - 1:
                    pool.tensor_tensor(logit[:, :, bass.ds(P * t, P)], lanesum[:, :, 0:P], lanesum[:, :, P:half],
                                       ALU.add).then_inc(s_add, 1)

            def step(t, q, tile=None, fields=()):
                c = Q * t + q
                items = items_of(c)
                mine = [k for k, (_, _, kind) in enumerate(items) if kind == G]
                start, summed = GATHER_PLACE if q == 2 else 0, SUM_PLACE
                fields = list(fields)
                for n, k in enumerate(mine):
                    if n == summed and (not isinstance(c, int) or c > 0):
                        lane_sums(*((t, q - 1) if q else (t - 1, Q - 1)))
                    if n == start and fields:
                        pool.wait_ge(s_ids, 16 * (tile + 1))
                        pool.nop(nofuse=True)
                        pool.wait_ge(s_split, tile)
                        pool.nop(nofuse=True)
                    make_lo(pool, pool.tensor_tensor, c, q, k, s_log)
                    if n >= start and fields:
                        take = -(-len(fields) // (len(mine) - n))
                        gather(tile, fields[:take])
                        fields = fields[take:]
                assert not fields

            quarters = [range(F * i // 4, F * (i + 1) // 4) for i in range(4)]
            pool.wait_ge(s_ids, 16)
            gather(0, range(F))
            step(0, 0, 1, range(0, F // 2))
            step(0, 1, 1, range(F // 2, F))
            with pool.Fori(0, BT - 2) as t:
                step(t, 2, t + 2, quarters[0])
                step(t, 3, t + 2, quarters[1])
                step(t + 1, 0, t + 2, quarters[2])
                step(t + 1, 1, t + 2, quarters[3])
            step(BT - 2, 2)
            step(BT - 2, 3)
            for q in range(Q - 1):
                step(BT - 1, q)
            step(BT - 1, Q - 1)
            lane_sums(BT - 1, Q - 1)

        @block.vector
        def _(dve):
            def split(t):
                dve.wait_ge(s_gather, 16 * F * (t + 1))
                for i in range(PARTS):
                    part = parts[:, :, F * i:F * (i + 1)].rearrange("p d f -> p f d")
                    if i:
                        dve.wait_ge(s_step, 5 * t + 2 * i)
                    nc.vector.tensor_copy(part, emb[:, :, :]).then_inc(s_step, 1)
                    dve.wait_ge(s_step, 5 * t + 2 * i + 1)
                    if i < PARTS - 1:
                        nc.vector.tensor_tensor(emb[:, :, :], emb[:, :, :], part, ALU.subtract) \
                            .then_inc(s_step, 1)
                nc.vector.sem_inc(s_split, 1)

            def wait_prod_free(c, k):
                past = back(c, k, PRODS)
                if past is None:
                    return
                if items_of(past[0])[past[1]][2] == WHOLE:
                    dve.wait_ge(s_used, upto(*past))
                else:
                    wait_lo(dve, *past)

            def twice(x):
                return x[:, None, :].broadcast_to([P, 2, CHUNK])

            def rotate(n, j, slot):
                dve.wait_ge(s_stack, n + 1)
                dve.wait_ge(s_sel, I0 * n + j + 1)
                tiles = len(TILES0[j])
                nc.vector.tensor_tensor(prod[:, slot, 0:tiles, :], twice(x0stack)[:, 0:tiles, :],
                                        ps_sel[:, 0:tiles, :], ALU.mult).then_inc(s_prod, 1)

            def product(c, q, k):
                layer, j, _ = items_of(c)[k]
                slot = prod_slot(c, k)
                wait_prod_free(c, k)
                if layer == 0:
                    rotate(c + 1, j, slot)
                    return
                chunk, parity, maps, made = c, q % 2, maps1, s_maps1
                if layer == 2:
                    maps, made = maps2, s_maps2
                    if j >= HEAD2 and k < at(c, 2, 0):
                        chunk, parity = c - 1, (q + 1) % 2
                if j == 0:
                    dve.wait_ge(made, 2 * (c + 1))
                dve.wait_ge(s_rep[j], 32 * (chunk + 1))
                nc.vector.tensor_tensor(prod[:, slot, :, :], pair(parity, j), twice(maps), ALU.mult) \
                    .then_inc(s_prod, 1)

            def step(t, q, late, split_next=False):
                c = Q * t + q
                items = items_of(c)
                for k, (layer, j, kind) in enumerate(items):
                    waits = items is LAST_ITEMS and (layer, j) == (2, 0)
                    while late and (late[0][3] <= k or waits):
                        ago, q1, k1, _ = late.pop(0)
                        make_lo(dve, nc.vector.tensor_tensor, c - ago, q1, k1, s_lov)
                    product(c, q, k)
                    if kind == V:
                        late.append((0, q, k, k + LAG))
                    if k == SPLIT_PLACE and split_next:
                        dve.wait_ge(s_xt, c + 2)
                        split(t + 1)
                return [(ago + 1, q1, k1, due - len(items)) for ago, q1, k1, due in late]

            dve.wait_ge(s_cin_w, 16 * CIN_LOADS)
            nc.vector.tensor_tensor(w0_sb[:, :, :], stage0[:, 0, :, :], stage0[:, 1, :, :], ALU.add) \
                .then_inc(s_w0, 1)
            dve.wait_ge(s_whi, 1)
            nc.vector.tensor_tensor(w_lo[:, :, :, :], stage, w_hi[:, :, :, :].bitcast(F32),
                                    ALU.subtract).then_inc(s_wlo, 1)
            split(0)
            dve.wait_ge(s_w0, 1)
            for j in range(I0):
                rotate(0, j, j)
            late = []
            for q in range(Q):
                late = step(0, q, late, split_next=q == 2)
            with dve.Fori(1, BT - 1) as t:
                for q in range(Q):
                    late = step(t, q, late, split_next=q == 2)
            for q in range(Q):
                late = step(BT - 1, q, late)
            for _, q, k, _ in late:
                make_lo(dve, nc.vector.tensor_tensor, CHUNKS - 1, q, k, s_lov)

        @block.scalar
        def _(act):
            def x0_copy(n):
                act.wait_ge(s_xt, n + 1)
                wait_past(act, s_sel, I0 * n)
                nc.scalar.activation(x0parts[:, :], ps_xt[0:PARTS * F, :], ACT.Copy).then_inc(s_x0, 1)

            def stack_copy(n, made):
                act.wait_ge(s_sela, n + 1)
                wait_past(act, s_prod, made)
                wait_past(act, s_store, 16 * n)
                nc.scalar.activation(x0stack[:, :], ps_x[:, :], ACT.Copy).then_inc(s_stack, 1)

            def relu_maps(z, layer, rows, maps, contracted, done):
                act.wait_ge(s_used, contracted)
                for at in (0, HALF):
                    nc.scalar.activation(maps[at:at + HALF, :], z[rows:rows + HALF, :], ACT.Relu,
                                         bias=cb_sb[rows:rows + HALF, layer:layer + 1]).then_inc(done, 1)

            def relu_direct(z, layer, rows, parity, done):
                nc.scalar.activation(direct[rows:rows + HALF, parity, 0, :], z[rows:rows + HALF, :], ACT.Relu,
                                     bias=cb_sb[rows:rows + HALF, layer:layer + 1]).then_inc(done, 1)

            def relu2(c, parity, contracted):
                act.wait_ge(s_used, contracted)
                nc.scalar.activation(direct[:, parity, 1, :], ps_z2[:, :], ACT.Relu,
                                     bias=cb_sb[:, 2:3]).then_inc(s_direct2, 1)

            def round_hi(c, q, k):
                act.wait_ge(s_prod, upto(c, k))
                wait_split_free(act, c, k, HIS)
                nc.scalar.activation(hi[:, split_slot(q, c, k, HIS), :, :], prod[:, prod_slot(c, k), :, :],
                                     ACT.Copy).then_inc(s_hi, 1)

            def step(t, q):
                c = Q * t + q
                items = items_of(c)
                more, first = items is not LAST_ITEMS, items is FIRST_ITEMS
                head = at(c, 2, 0)
                for k, (layer, j, kind) in enumerate(items):
                    if k == head:
                        if not first:
                            act.wait_ge(s_prod, upto(c, at(c, 2, I1 - 1)))
                        relu_maps(ps_z1, 1, HALF, maps2, upto(c, I1 - 1), s_maps2)
                    if kind != WHOLE:
                        round_hi(c, q, k)
                    if k == X0_PLACE and more:
                        x0_copy(c + 1)
                    if k == STACK_PLACE and more:
                        stack_copy(c + 1, before(c))
                    if k == head + 1:
                        relu_direct(ps_z1, 1, 0, q % 2, s_direct1)
                    if k == head + 2 and not first:
                        relu2(c - 1, (q + 1) % 2, upto(c, at(c, 2, I1 - 1)))
                    if k == head + 3 and more:
                        relu_maps(ps_z0, 0, 0, maps1, upto(c, at(c, 0, I0 - 1)), s_maps1)
                    if k == head + HEAD2 - 1 and more:
                        wait_past(act, s_sum, c)
                        relu_direct(ps_z0, 0, HALF, (q + 1) % 2, s_direct0)

            act.wait_ge(s_cin_w, 16 * CIN_LOADS)
            nc.scalar.activation(w_hi[:, :, :, :], stage, ACT.Copy).then_inc(s_whi, 1)
            x0_copy(0)
            stack_copy(0, 0)
            relu_maps(ps_z0, 0, 0, maps1, I0, s_maps1)
            relu_direct(ps_z0, 0, HALF, 0, s_direct0)
            for q in range(Q):
                step(0, q)
            with act.Fori(1, BT - 1) as t:
                for q in range(Q):
                    step(t, q)
            for q in range(Q):
                step(BT - 1, q)
            end = CHUNKS - 1
            relu2(end, end % 2, upto(end, len(LAST_ITEMS) - 1))

            act.wait_ge(s_mlp_c, 16 * 3)

            def mlp(n):
                for m in range(M1):
                    act.wait_ge(s_h1, M1 * n + m + 1)
                    if m == 0:
                        wait_past(act, s_h2, M2 * n)
                    nc.scalar.activation(hidden[:, m, :], ps_h1[m], ACT.Relu,
                                         bias=bt1_sb[:, m:m + 1]).then_inc(s_h1r, 1)
                for m, z in enumerate((ps_z0, ps_z1)):
                    act.wait_ge(s_h2, M2 * n + m + 1)
                    if m == 0:
                        wait_past(act, s_y, n)
                    nc.scalar.activation(hidden[:, M1 + m, :], z[:, :], ACT.Relu,
                                         bias=bt2_sb[:, m:m + 1]).then_inc(s_h2r, 1)
                act.wait_ge(s_y, n + 1)
                nc.scalar.activation(y_sb[0:1, bass.ds(NB * n, NB)], ps_z2[0:1, :], ACT.Copy).then_inc(s_yc, 1)

            mlp(0)
            with act.Fori(1, B // NB) as n:
                mlp(n)

        @block.tensor
        def _(pe):
            def transposes(n, q):
                wait_past(pe, s_stack, n)
                for d in range(LANES):
                    last = nc.tensor.transpose(ps_xt[0:PARTS * F, P * d:P * (d + 1)],
                                               parts[:, LANES * q + d, :], ident_sb[:, :])
                last.then_inc(s_xt, 1)

            def select_stack(n):
                pe.wait_ge(s_x0, n + 1)
                nc.tensor.matmul(ps_x[:, :], sel_sb[:, 0, :], x0parts[:, :], start=True, stop=True) \
                    .then_inc(s_sela, 1)

            def select(n, g, made):
                wait_past(pe, s_prod, made)
                for i, tile in enumerate(TILES0[g]):
                    last = nc.tensor.matmul(ps_sel[:, i, :], sel_sb[:, 1 + tile, :], x0parts[:, :],
                                            start=True, stop=True)
                last.then_inc(s_sel, 1)

            def whole(item, slot, w, tiles, z, first, final):
                pe.wait_ge(s_prod, item)
                for i, tile in enumerate(tiles):
                    last = nc.tensor.matmul(z[:, :], w[:, tile, :], prod[:, slot, i, :],
                                            start=first and i == 0, stop=final and i == len(tiles) - 1)
                last.then_inc(s_used, 1)

            def contract(c, q, k):
                layer, j, kind = items_of(c)[k]
                slot = prod_slot(c, k)
                z = (ps_z0, ps_z1, ps_z2)[layer]
                if j == 0:
                    wait_past(pe, (s_direct0, s_direct1, s_direct2)[layer], c + 1 if layer == 0 else c)
                if layer == 0:
                    whole(upto(c, k), slot, w0_sb, TILES0[j], z, j == 0, j == I0 - 1)
                    return
                if kind == WHOLE:
                    w, wholes = (w1_sb, WHOLE1) if layer == 1 else (w2_sb, WHOLE2)
                    tile = 2 * wholes.index(j)
                    whole(upto(c, k), slot, w, (tile, tile + 1), z, j == 0, j == I1 - 1)
                    return
                hi_slot, lo_slot = split_slot(q, c, k, HIS), split_slot(q, c, k, LOS)
                row = SPLIT1.index(j) if layer == 1 else len(SPLIT1) + SPLIT2.index(j)
                pe.wait_ge(s_hi, upto(c, k, (V, G)))
                for i in range(2):
                    for w in (w_lo, w_hi):
                        nc.tensor.matmul(z[:, :], w[:, row, i, :], hi[:, hi_slot, i, :],
                                         start=j == 0 and i == 0 and w is w_lo, stop=False)
                wait_lo(pe, c, k)
                for i in range(2):
                    last = nc.tensor.matmul(z[:, :], w_hi[:, row, i, :], lo[:, lo_slot, i, :],
                                            start=False, stop=j == I1 - 1 and i == 1)
                last.then_inc(s_used, 1)

            def step(t, q):
                c = Q * t + q
                items = items_of(c)
                more = items is not LAST_ITEMS
                if more:
                    if q == Q - 1:
                        pe.wait_ge(s_split, t + 2)
                    transposes(c + 1, (q + 1) % Q)
                for k in range(len(items)):
                    if more and k == SELECT_STACK_PLACE:
                        select_stack(c + 1)
                    for g in range(I0 if more else 0):
                        if k == at(c, 0, g) - SELECT_AHEAD:
                            select(c + 1, g, upto(c, at(c, 0, g - 1)) if g else before(c))
                    contract(c, q, k)

            pe.wait_ge(s_cin_w, 16 * CIN_LOADS)
            pe.wait_ge(s_split, 1)
            transposes(0, 0)
            select_stack(0)
            for g in range(I0):
                select(0, g, g)
            pe.wait_ge(s_w0, 1)
            for k in range(I0):
                contract(-1, 0, k)
            pe.wait_ge(s_wlo, 1)
            for q in range(Q):
                step(0, q)
            with pe.Fori(1, BT - 1) as t:
                for q in range(Q):
                    step(t, q)
            for q in range(Q):
                step(BT - 1, q)

            pe.wait_ge(s_mlp_c, 16 * 3)
            pe.wait_ge(s_mlp_w, 16 * 3)
            pe.wait_ge(s_add, ADDS * BT)
            pe.wait_ge(s_direct2, CHUNKS)

            def mlp(n):
                cols = bass.ds(NB * n, NB)
                wait_past(pe, s_h1r, M1 * n)
                for m in range(M1):
                    ms = slice(P * m, P * (m + 1))
                    for k in range(2):
                        nc.tensor.matmul(ps_h1[m], wt1_sb[:, k, ms], logit[:, k, cols], start=k == 0, stop=False)
                    nc.tensor.matmul(ps_h1[m], wt1d_sb[:, ms], dense_sb[:, cols], start=False, stop=True) \
                        .then_inc(s_h1, 1)
                pe.wait_ge(s_wt2, 16)
                wait_past(pe, s_h2r, M2 * n)
                for m, z in enumerate((ps_z0, ps_z1)):
                    for k in range(M1):
                        pe.wait_ge(s_h1r, M1 * n + k + 1)
                        last = nc.tensor.matmul(z[:, :], wt2_sb[:, k, P * m:P * (m + 1)], hidden[:, k, :],
                                                start=k == 0, stop=k == M1 - 1)
                    last.then_inc(s_h2, 1)
                wait_past(pe, s_yc, n)
                for k in range(M2):
                    pe.wait_ge(s_h2r, M2 * n + k + 1)
                    last = nc.tensor.matmul(ps_z2[0:1, :], wt3_sb[:, k:k + 1], hidden[:, M1 + k, :],
                                            start=k == 0, stop=k == M2 - 1)
                last.then_inc(s_y, 1)

            mlp(0)
            with pe.Fori(1, B // NB) as n:
                mlp(n)


def kernel(**inputs):
    import ml_dtypes
    import numpy as np
    import concourse.bacc as bacc
    from concourse.bass_utils import run_bass_kernel_spmd as run

    f32 = np.float32
    x = {k: np.asarray(v) for k, v in inputs.items()}

    w0 = x["L0_rec_w0"]
    w0a, w0b = np.zeros((P, T0, S), f32), np.zeros((P, T0, S), f32)
    sel = np.zeros((PARTS * F, 2 * I0, P), ml_dtypes.bfloat16)
    h = np.arange(F)
    rows = [part * F for part in range(PARTS)]
    for i in range(ROT):
        for r0 in rows:
            sel[r0 + h, 0, i * F + h] = 1
    for n, r in enumerate(ROTATIONS):
        t, i = divmod(n, ROT)
        k = (h + r) % F
        w0a[i * F + h, t] = w0[h, k]
        if r:
            w0b[i * F + h, t] = w0[k, h]
        for r0 in rows:
            sel[r0 + k, 1 + t, i * F + h] = 1

    def pairs(w):
        full = np.zeros((2 * T1, HALF, S), f32)
        full[:F] = w
        return np.ascontiguousarray(full.reshape(T1, P, S).transpose(1, 0, 2))

    swap = np.r_[HALF:S, 0:HALF]
    w1, w2 = pairs(x["L0_rec_w1"][:, :, swap]), pairs(x["L0_rec_w2"])

    def tiles(w, items):
        return np.ascontiguousarray(w[:, [2 * j + i for j in items for i in range(2)]])

    cin_bias = np.stack([x["L0_rec_b0"], x["L0_rec_b1"][swap], x["L0_rec_b2"]], axis=1)
    wt1 = x["W_top1"][np.r_[swap, S:S + S + DENSE]]
    arrays = {
        "ids": np.ascontiguousarray(x["ids"].reshape(BT, P, F)),
        "dense_t": np.ascontiguousarray(x["dense_ctx"].T),
        "sel": sel,
        "ident": np.eye(P, dtype=ml_dtypes.bfloat16),
        "w0a": w0a,
        "w0b": w0b,
        "w1_whole": tiles(w1, WHOLE1),
        "w2_whole": tiles(w2, WHOLE2),
        "w_split": np.concatenate([tiles(w1, SPLIT1), tiles(w2, SPLIT2)], axis=1),
        "cin_bias": np.ascontiguousarray(cin_bias),
        "wt1": np.ascontiguousarray(wt1),
        "bt1": np.ascontiguousarray(x["b_top1"].reshape(M1, P).T),
        "wt2": x["W_top2"],
        "bt2": np.ascontiguousarray(x["b_top2"].reshape(M2, P).T),
        "wt3": np.ascontiguousarray(x["W_top3"].reshape(M2, P).T),
    }
    tables = {f"tbl_{f}": x[f"tbl_{f}"] for f in range(F)}

    nc = bacc.Bacc("TRN2", target_bir_lowering=False, num_devices=1)

    def dram(name, a):
        return nc.dram_tensor(name, a.shape, mybir.dt.from_np(a.dtype), kind="ExternalInput").ap()

    tbl_aps = [dram(f"tbl_{f}", tables[f"tbl_{f}"]) for f in range(F)]
    aps = {name: dram(name, a) for name, a in arrays.items()}
    out = nc.dram_tensor("out", (B, 1), F32, kind="ExternalOutput").ap()
    x0rows = nc.dram_tensor("x0rows", (2, 2 * T1, CHUNK), F32, kind="Internal").ap()
    dlrm_tower(nc, tbl_aps, x0rows=x0rows, out=out, **aps)
    arrays.update(tables)
    r = run(nc, [arrays], core_ids=[0])
    return r.results[0]["out"]
```

```python
from contextlib import ExitStack

import concourse.bass as bass
from concourse import mybir

P = 128
B = 2048
F = 39
D = 16
S = 128
HALF = S // 2
BT = B // P
LANES = 4
Q = D // LANES
CHUNK = LANES * P
CHUNKS = BT * Q
ROT = 3
ROWS0 = ROT * F
ROTATIONS = list(range((F + 1) // 2))
T0 = -(-len(ROTATIONS) // ROT)
ROWS = F + ROT * T0
T1 = (F + 1) // 2
I0 = (T0 + 1) // 2
TILES0 = [tuple(range(2 * j, min(2 * j + 2, T0))) for j in range(I0)]
I1 = T1 // 2
PRODS = 8
HIS = 6
LOS = 4
SPREAD_PLACE = 5
TRANSPOSE_PLACE = 13
STACK_PLACE = 19
DIRECT1_PLACE = 0
RELU2_PLACE = 5
MAPS1_PLACE = 5
DIRECT0_PLACE = 6
STORE_PAIR = 4
GATHER_PLACE = 2
SUM_PLACE = 8
EARLY = 21
LAG = 5
H1 = 512
H2 = 256
DENSE = 16
M1 = H1 // P
M2 = H2 // P
NB = 512
BLOCKS = B // NB

ALU = mybir.AluOpType
ACT = mybir.ActivationFunctionType
F32 = mybir.dt.float32
I32 = mybir.dt.int32
F32R = mybir.dt.float32r

WHOLE, V, G = "whole", "V", "G"
KINDS1 = [WHOLE, G, WHOLE, V, V, G, WHOLE, G, V, G]
KINDS2 = [G, V, G, WHOLE, V, WHOLE, G, V, G, G]
MID = "T0T0T00"
HEAD2 = I1 - MID.count("T")
LAYER1 = [(1, j, kind) for j, kind in enumerate(KINDS1)]
LAYER0 = [(0, j, WHOLE) for j in range(I0)]
LAYER2 = [(2, j, kind) for j, kind in enumerate(KINDS2)]
HEAD, TAIL = LAYER2[:HEAD2], LAYER2[HEAD2:]
MIDDLE = [(TAIL if x == "T" else LAYER0)[MID[:i].count(x)] for i, x in enumerate(MID)]
ITEMS = LAYER1 + MIDDLE + HEAD
FIRST_ITEMS = LAYER1 + LAYER0 + HEAD
LAST_ITEMS = LAYER1 + TAIL + HEAD + TAIL
TWICE = len(TAIL)


def count(items, kinds):
    return sum(kind in kinds for _, _, kind in items)


NI = len(ITEMS)
NS = count(ITEMS, (V, G))
WHOLE1, WHOLE2 = ([j for _, j, kind in layer if kind == WHOLE] for layer in (LAYER1, LAYER2))
SPLIT1, SPLIT2 = ([j for _, j, kind in layer if kind != WHOLE] for layer in (LAYER1, LAYER2))
ALL = (WHOLE, V, G)

assert Q % 2 == 0 and NI % PRODS == 0 and NS * Q % HIS == 0 and NS * Q % LOS == 0 and len(TAIL) == 3
assert 2 * H1 <= len(SPLIT1) * 2 * S and M1 * H2 <= len(SPLIT2) * 2 * S


def wait_past(eng, sem, value):
    if not isinstance(value, int) or value > 0:
        eng.wait_ge(sem, value)


def before(c, kinds=ALL):
    start = count(LAYER0, kinds)
    if isinstance(c, int) and c == 0:
        return start
    return start + count(FIRST_ITEMS, kinds) + count(ITEMS, kinds) * (c - 1)


def items_of(c):
    if isinstance(c, int):
        return LAYER0 if c < 0 else FIRST_ITEMS if c == 0 else LAST_ITEMS if c == CHUNKS - 1 else ITEMS
    return ITEMS


def upto(c, k, kinds=ALL):
    own = count(items_of(c)[:k + 1], kinds)
    return own if isinstance(c, int) and c < 0 else before(c, kinds) + own


def at(c, layer, j, late=False):
    where = [k for k, item in enumerate(items_of(c)) if item[:2] == (layer, j)]
    return where[-1 if late else 0]


def place(items, k):
    return k - len(TAIL) if items is FIRST_ITEMS else k


def back(c, k, n, kinds=ALL):
    while True:
        for i in range(k - 1, -1, -1):
            n -= items_of(c)[i][2] in kinds
            if n == 0:
                return c, i
        if isinstance(c, int) and c < 0:
            return None
        c, k = c - 1, len(items_of(c - 1))


def dlrm_tower(nc, tables, ids, dense_t, ident, w0a, w0b, w1_whole, w2_whole, w_split, cin_bias, wt1, bt1,
               wt2, bt2, wt3, x0rows, logits, out):
    with ExitStack() as ctx:
        def sb(name, shape, dt=F32):
            return ctx.enter_context(nc.sbuf_tensor(name, shape, dt))

        def ps(name, shape, dt=F32):
            return ctx.enter_context(nc.psum_tensor(name, shape, dt))

        def sem(name):
            return ctx.enter_context(nc.semaphore(name))

        ident_sb = sb("ident_sb", [P, P])
        w0_sb = sb("w0_sb", [P, T0, S])
        w1_sb = sb("w1_sb", [P, 2 * len(WHOLE1), S])
        w2_sb = sb("w2_sb", [P, 2 * len(WHOLE2), S])
        w_hi = sb("w_hi", [P, NS, 2, S], F32R)
        w_lo = sb("w_lo", [P, NS, 2, S], F32R)
        cb_sb = sb("cb_sb", [P, 3])
        wt3_sb = sb("wt3_sb", [P, M2])
        bt1_sb = sb("bt1_sb", [P, M1])
        bt2_sb = sb("bt2_sb", [P, M2])
        ids_sb = sb("ids_sb", [P, F], I32)
        emb = sb("emb", [P, F, D])
        emb_rot = sb("emb_rot", [P, D, ROWS0])
        x0stack = sb("x0stack", [ROWS0, CHUNK])
        x0rot = sb("x0rot", [P, T0, CHUNK])
        x0rep = sb("x0rep", [P, TWICE + I1, 2, CHUNK])
        prod = sb("prod", [P, PRODS, 2, CHUNK])
        hi = sb("hi", [P, HIS, 2, CHUNK], F32R)
        lo = sb("lo", [P, LOS, 2, CHUNK], F32R)
        direct = sb("direct", [P, 2, 2, CHUNK])
        lanesum = sb("lanesum", [P, 2, CHUNK // 2])
        logit = sb("logit", [P, 2, P])

        ps_h = ps("ps_h", [P, 2, CHUNK])
        maps1 = ps("maps1", [P, CHUNK])
        maps2 = ps("maps2", [P, CHUNK])
        ps_z0 = ps("ps_z0", [P, CHUNK])
        ps_z1 = ps("ps_z1", [P, CHUNK])
        ps_z2 = ps("ps_z2", [P, CHUNK])
        ps_x = ps("ps_x", [P, CHUNK])

        stage0 = prod[:, 0:2, :, :].rearrange("p a b n -> p (a b n)")[:, 0:2 * T0 * S] \
            .rearrange("p (a g m) -> p a g m", a=2, m=S)
        stage = x0rep[:, 0:5, :, :].rearrange("p a b n -> p (a b n)")[:, 0:NS * 2 * S] \
            .rearrange("p (k g m) -> p k g m", g=2, m=S)
        once = x0rep[:, I1 - TWICE:I1, :, :].rearrange("p a b n -> p (a b n)")
        dense_sb = once[0:DENSE, 0:B]
        wt1_sb = once[:, B:B + 2 * H1].rearrange("p (k m) -> p k m", k=2)
        wt2_sb = x0rot[:, 0:2, :].rearrange("p a n -> p (a n)").rearrange("p (k m) -> p k m", k=M1)
        wt1d_sb = x0rot[0:DENSE, 2, 0:H1]
        all_logits = x0rep[:, 3:I1 - TWICE, :, :].rearrange("p a b n -> p (a b n)") \
            .rearrange("p (k n) -> p k n", k=2)
        hidden = x0rep[:, 0:3, :, :].rearrange("p a b n -> p (a b) n")
        y_sb = direct[0:1, :, :, :].rearrange("p a b n -> p (a b n)")
        w1_hi, w1_lo = (w[:, 0:2 * H1 // (2 * S), :, :].rearrange("p k g m -> p (k g m)")
                        .rearrange("p (k m) -> p k m", k=2) for w in (w_hi, w_lo))
        w2_hi, w2_lo = (w[:, NS - M1 * H2 // (2 * S):, :, :].rearrange("p k g m -> p (k g m)")
                        .rearrange("p (k m) -> p k m", k=M1) for w in (w_hi, w_lo))
        logit_hi, logit_lo = hi[:, 0, :, :], lo[:, 0, :, :]
        hidden_hi, hidden_lo = (x[:, 2:4, :, :].rearrange("p a b n -> p (a b) n") for x in (hi, lo))
        ps_h1 = (ps_h[:, 0, :], ps_h[:, 1, :], maps1[:, :], maps2[:, :])

        s_ids = sem("s_ids")
        s_cin_w = sem("s_cin_w")
        s_mlp_c = sem("s_mlp_c")
        s_mlp_w = sem("s_mlp_w")
        s_spill = sem("s_spill")
        s_reload = sem("s_reload")
        s_store = sem("s_store")
        s_rot_start = sem("s_rot_start")
        s_rot = sem("s_rot")
        s_rep = [sem(f"s_rep{j}") for j in range(I1)]
        s_gather = sem("s_gather")
        s_w0 = sem("s_w0")
        s_whi = sem("s_whi")
        s_wlo = sem("s_wlo")
        s_spread = sem("s_spread")
        s_xt = sem("s_xt")
        s_stack = sem("s_stack")
        s_prod = sem("s_prod")
        s_hi = sem("s_hi")
        s_lov = sem("s_lov")
        s_log = sem("s_log")
        s_used = sem("s_used")
        s_maps1 = sem("s_maps1")
        s_maps2 = sem("s_maps2")
        s_direct0 = sem("s_direct0")
        s_direct1 = sem("s_direct1")
        s_direct2 = sem("s_direct2")
        s_add = sem("s_add")
        s_sum = sem("s_sum")
        s_h1 = sem("s_h1")
        s_h1r = sem("s_h1r")
        s_h1_lo = sem("s_h1_lo")
        s_mlp_hi = sem("s_mlp_hi")
        s_mlp_lo = sem("s_mlp_lo")
        s_logit_hi = sem("s_logit_hi")
        s_logit_lo = sem("s_logit_lo")
        s_h2 = sem("s_h2")
        s_h2r = sem("s_h2r")
        s_y = sem("s_y")
        s_yc = sem("s_yc")
        s_out = sem("s_out")

        CIN_LOADS = 7
        ADDS = 2 * Q
        block = ctx.enter_context(nc.Block())

        def pair(parity, j):
            return x0rep[:, j + (TWICE if parity and j >= HEAD2 else 0), :, :]

        def wait_lo(eng, c, k):
            kind = items_of(c)[k][2]
            eng.wait_ge(s_lov if kind == V else s_log, upto(c, k, (kind,)))

        def wait_split_free(eng, c, k, buffers):
            past = back(c, k, buffers, (V, G))
            if past:
                eng.wait_ge(s_used, upto(*past))

        def prod_slot(c, k):
            if isinstance(c, int) and c < 0:
                return k
            return (before(0 if isinstance(c, int) and c == 0 else 1) + k) % PRODS

        def split_slot(q, c, k, buffers):
            own = count(items_of(c)[:k], (V, G))
            return (before(c if isinstance(c, int) and c == 0 else Q + q, (V, G)) + own) % buffers

        def make_lo(eng, op, c, q, k, done):
            eng.wait_ge(s_hi, upto(c, k, (V, G)))
            wait_split_free(eng, c, k, LOS)
            op(lo[:, split_slot(q, c, k, LOS), :, :], prod[:, prod_slot(c, k), :, :],
               hi[:, split_slot(q, c, k, HIS), :, :].bitcast(F32),
               ALU.subtract).then_inc(done, 1)

        @block.sync
        def _(sp):
            def store_rows(n, parity):
                sp.wait_ge(s_stack, n + 1)
                sp.nop(nofuse=True)
                if not isinstance(n, int) or n > 1:
                    sp.wait_ge(s_prod, upto(n - 2, I1 - 1))
                    sp.nop(nofuse=True)
                for at_row, rows in ((0, F), (F, ROWS - F)):
                    sp.dma_start(x0rows[parity, at_row:at_row + rows, :], x0stack[0:rows, :]).then_inc(s_store, 16)

            def rotations(n, parity):
                sp.wait_ge(s_store, 32 * (n + 1))
                sp.nop(nofuse=True)
                if not isinstance(n, int) or n > 0:
                    c = n - 2
                    sp.wait_ge(s_prod, upto(c, at(c, 0, I0 - 1)))
                    sp.nop(nofuse=True)
                start = isinstance(n, int) and n == 0
                groups = ((0, 2, s_rot_start), (2, T0 - 2, s_rot)) if start else ((0, T0, s_rot),)
                for first, tiles, landed in groups:
                    for i in range(ROT):
                        rows = x0rows[parity, ROT * first + i:ROT * first + i + 1, :]
                        rows = bass.AP(rows.tensor, rows.offset, [[CHUNK, F], [ROT * CHUNK, tiles], [1, CHUNK]])
                        sp.dma_start(x0rot[F * i:F * (i + 1), first:first + tiles, :], rows).then_inc(landed, 16)

            def replicate(n, parity, then=False):
                c = n - 1
                for j in list(range(HEAD2, I1)) + list(range(HEAD2)):
                    if then and j == STORE_PAIR:
                        store_rows(n + 1, 1 - parity)
                    if (not isinstance(n, int) or n > 0) and (2, j) in [x[:2] for x in items_of(c)]:
                        sp.wait_ge(s_prod, upto(c, at(c, 2, j)))
                        sp.nop(nofuse=True)
                    for i in range(2):
                        rows = x0rows[parity, 4 * j + i:4 * j + i + 3:2, :]
                        sp.dma_start(pair(parity, j)[HALF * i:HALF * (i + 1), :, :],
                                     rows[None, :, :].broadcast_to([HALF, 2, CHUNK])).then_inc(s_rep[j], 16)
                if then:
                    rotations(n + 1, 1 - parity)

            def spill(t):
                sp.wait_ge(s_add, ADDS * (t + 1))
                sp.nop(nofuse=True)
                sp.dma_start(logits[:, :, bass.ds(P * t, P)], logit[:, :, :]).then_inc(s_spill, 16)

            def load_ids(t):
                sp.wait_ge(s_gather, 16 * F * t)
                sp.nop(nofuse=True)
                sp.dma_start(ids_sb[:, :], ids[bass.ds(t, 1), :, :].rearrange("o p f -> (o p) f")) \
                    .then_inc(s_ids, 16)

            def step(t, q):
                c = Q * t + q
                replicate(c + 1, (q + 1) % 2, items_of(c + 1) is not LAST_ITEMS)

            sp.dma_start(ids_sb[:, :], ids[0]).then_inc(s_ids, 16)
            for dst, src in ((stage, w_split.rearrange("p (k g) m -> p k g m", g=2)),
                             (stage0[:, 0, :, :], w0a), (stage0[:, 1, :, :], w0b),
                             (ident_sb[:, :], ident), (w1_sb[:, :, :], w1_whole),
                             (w2_sb[:, :, :], w2_whole), (cb_sb[:, :], cin_bias)):
                sp.dma_start(dst, src).then_inc(s_cin_w, 16)
            for dst, src in ((wt3_sb[:, :], wt3), (bt1_sb[:, :], bt1), (bt2_sb[:, :], bt2)):
                sp.dma_start(dst, src).then_inc(s_mlp_c, 16)
            load_ids(1)
            sp.wait_ge(s_wlo, 1)
            store_rows(0, 0)
            rotations(0, 0)
            replicate(0, 0, then=True)
            step(0, 0)
            step(0, 1)
            with sp.Fori(0, BT - 2) as t:
                load_ids(t + 2)
                for q in range(2, Q):
                    step(t, q)
                step(t + 1, 0)
                spill(t)
                step(t + 1, 1)
            for q in range(2, Q):
                step(BT - 2, q)
            step(BT - 1, 0)
            spill(BT - 2)
            for q in range(1, Q - 1):
                step(BT - 1, q)

            end = CHUNKS - 1
            sp.wait_ge(s_prod, upto(end, at(end, 2, I1 - 1)))
            sp.dma_start(dense_sb, dense_t).then_inc(s_mlp_w, 16)
            sp.dma_start(wt1_sb, wt1[0:2 * P, :].rearrange("(k p) m -> p k m", p=P)).then_inc(s_mlp_w, 16)
            sp.dma_start(wt1d_sb, wt1[2 * P:, :]).then_inc(s_mlp_w, 16)
            sp.dma_start(wt2_sb, wt2.rearrange("(k p) m -> p k m", p=P)).then_inc(s_mlp_w, 16)
            sp.wait_ge(s_spill, 16 * (BT - 1))
            sp.wait_ge(s_prod, upto(end, at(end, 2, HEAD2 - 1)))
            sp.dma_start(all_logits[:, :, 0:P * (BT - 1)], logits[:, :, 0:P * (BT - 1)]).then_inc(s_reload, 16)
            sp.wait_ge(s_yc, BLOCKS)
            sp.dma_start(out.rearrange("b o -> o b"), y_sb).then_inc(s_out, 16)
            sp.wait_ge(s_out, 16)

        @block.gpsimd
        def _(pool):
            def gather(t, fields):
                for f in fields:
                    pool.indirect_dma_start(
                        emb[:, f, :], None, tables[f][:, :],
                        bass.IndirectOffsetOnAxis(ap=ids_sb[:, f:f + 1], axis=0)).then_inc(s_gather, 16)

            def lane_sums(t, q):
                c, half = Q * t + q, CHUNK // 2
                r = direct[:, q % 2, :, :]
                pool.wait_ge(s_direct0, c + 1)
                pool.wait_ge(s_direct1, c + 1)
                pool.wait_ge(s_direct2, c + 1)
                done = ADDS * t + (2 * q - 1 if q else 0)
                wait_past(pool, s_add, done)
                if q == 0:
                    pool.tensor_tensor(lanesum[:, :, :], r[:, :, 0:half], r[:, :, half:], ALU.add) \
                        .then_inc(s_add, 1)
                    pool.wait_ge(s_add, done + 1)
                else:
                    pool.tensor_tensor(lanesum[:, :, :], lanesum[:, :, :], r[:, :, 0:half], ALU.add) \
                        .then_inc(s_add, 1)
                    pool.wait_ge(s_add, done + 1)
                    pool.tensor_tensor(lanesum[:, :, :], lanesum[:, :, :], r[:, :, half:], ALU.add) \
                        .then_inc(s_add, 1)
                    pool.wait_ge(s_add, done + 2)
                pool.sem_inc(s_sum, 1)
                if q == Q - 1:
                    last = isinstance(t, int) and t == BT - 1
                    if last:
                        pool.wait_ge(s_prod, upto(c, at(c, 2, HEAD2 - 1)))
                    else:
                        wait_past(pool, s_spill, 16 * t)
                    pool.tensor_tensor(all_logits[:, :, P * t:] if last else logit[:, :, :],
                                       lanesum[:, :, 0:P], lanesum[:, :, P:half], ALU.add).then_inc(s_add, 1)

            def step(t, q, tile=None, fields=()):
                c = Q * t + q
                items = items_of(c)
                mine = [k for k, (_, _, kind) in enumerate(items) if kind == G]
                start, summed = GATHER_PLACE if q == 2 else 0, SUM_PLACE
                fields = list(fields)
                for n, k in enumerate(mine):
                    if n == summed and (not isinstance(c, int) or c > 0):
                        lane_sums(*((t, q - 1) if q else (t - 1, Q - 1)))
                    if n == start and fields and not (isinstance(c, int) and c < 2):
                        pool.wait_ge(s_ids, 16 * (tile + 1))
                        pool.nop(nofuse=True)
                        pool.wait_ge(s_spread, ROT * tile)
                        pool.nop(nofuse=True)
                    make_lo(pool, pool.tensor_tensor, c, q, k, s_log)
                    if n >= start and fields:
                        take = -(-len(fields) // (len(mine) - n))
                        gather(tile, fields[:take])
                        fields = fields[take:]
                assert not fields

            quarters = [range(F * i // 4, F * (i + 1) // 4) for i in range(4)]
            pool.wait_ge(s_ids, 16)
            gather(0, range(F))
            pool.wait_ge(s_ids, 32)
            pool.wait_ge(s_spread, ROT)
            gather(1, range(EARLY))
            step(0, 0, 1, range(EARLY, (EARLY + F) // 2))
            step(0, 1, 1, range((EARLY + F) // 2, F))
            with pool.Fori(0, BT - 2) as t:
                step(t, 2, t + 2, quarters[0])
                step(t, 3, t + 2, quarters[1])
                step(t + 1, 0, t + 2, quarters[2])
                step(t + 1, 1, t + 2, quarters[3])
            step(BT - 2, 2)
            step(BT - 2, 3)
            for q in range(Q - 1):
                step(BT - 1, q)
            step(BT - 1, Q - 1)
            lane_sums(BT - 1, Q - 1)

        @block.vector
        def _(dve):
            def wait_prod_free(c, k):
                past = back(c, k, PRODS)
                if past is None:
                    return
                if items_of(past[0])[past[1]][2] == WHOLE:
                    dve.wait_ge(s_used, upto(*past))
                else:
                    wait_lo(dve, *past)

            def twice(x):
                return x[:, None, :].broadcast_to([P, 2, CHUNK])

            def rotate(n, j, slot):
                if j == 0:
                    dve.wait_ge(s_stack, n + 1)
                start = isinstance(n, int) and n == 0
                if start and j == 0:
                    dve.wait_ge(s_rot_start, 16 * ROT)
                if j == (1 if start else 0):
                    dve.wait_ge(s_rot, 16 * ROT * (n + 1))
                tiles = len(TILES0[j])
                nc.vector.tensor_tensor(prod[0:ROWS0, slot, 0:tiles, :],
                                        x0stack[:, None, :].broadcast_to([ROWS0, tiles, CHUNK]),
                                        x0rot[0:ROWS0, 2 * j:2 * j + tiles, :], ALU.mult).then_inc(s_prod, 1)

            def product(c, q, k):
                layer, j, _ = items_of(c)[k]
                slot = prod_slot(c, k)
                wait_prod_free(c, k)
                if layer == 0:
                    rotate(c + 1, j, slot)
                    return
                chunk, parity, maps, made = c, q % 2, maps1, s_maps1
                if layer == 2:
                    maps, made = maps2, s_maps2
                    if j >= HEAD2 and k < at(c, 2, 0):
                        chunk, parity = c - 1, (q + 1) % 2
                if j == 0:
                    dve.wait_ge(made, 2 * (c + 1))
                dve.wait_ge(s_rep[j], 32 * (chunk + 1))
                nc.vector.tensor_tensor(prod[:, slot, :, :], pair(parity, j), twice(maps), ALU.mult) \
                    .then_inc(s_prod, 1)

            def step(t, q, late):
                c = Q * t + q
                items = items_of(c)
                for k, (layer, j, kind) in enumerate(items):
                    waits = items is LAST_ITEMS and (layer, j) == (2, 0)
                    while late and (late[0][3] <= k or waits):
                        ago, q1, k1, _ = late.pop(0)
                        make_lo(dve, nc.vector.tensor_tensor, c - ago, q1, k1, s_lov)
                    product(c, q, k)
                    if kind == V:
                        late.append((0, q, k, k + LAG))
                return [(ago + 1, q1, k1, due - len(items)) for ago, q1, k1, due in late]

            dve.wait_ge(s_cin_w, 16 * CIN_LOADS)
            nc.vector.tensor_tensor(w0_sb[:, :, :], stage0[:, 0, :, :], stage0[:, 1, :, :], ALU.add) \
                .then_inc(s_w0, 1)
            dve.wait_ge(s_whi, 1)
            nc.vector.tensor_tensor(w_lo[:, :, :, :], stage, w_hi[:, :, :, :].bitcast(F32),
                                    ALU.subtract).then_inc(s_wlo, 1)
            dve.wait_ge(s_w0, 1)
            for j in range(I0):
                rotate(0, j, j)
            late = []
            for q in range(Q):
                late = step(0, q, late)
            with dve.Fori(1, BT - 1) as t:
                for q in range(Q):
                    late = step(t, q, late)
            for q in range(Q):
                late = step(BT - 1, q, late)
            end = CHUNKS - 1
            for _, q, k, _ in late:
                make_lo(dve, nc.vector.tensor_tensor, end, q, k, s_lov)

            def subtract(dst, x, x_hi, done):
                nc.vector.tensor_tensor(dst, x, x_hi.bitcast(F32), ALU.subtract).then_inc(done, 1)

            dve.wait_ge(s_mlp_hi, 1)
            subtract(w1_lo, wt1_sb, w1_hi, s_mlp_lo)
            dve.wait_ge(s_mlp_hi, 2)
            subtract(w2_lo, wt2_sb, w2_hi, s_mlp_lo)

            def mlp(n):
                wait_past(dve, s_h2, M2 * n)
                for m in range(M1):
                    dve.wait_ge(s_h1r, 2 * (M1 * n + m + 1))
                    subtract(hidden_lo[:, m, :], hidden[:, m, :], hidden_hi[:, m, :], s_h1_lo)
                if not isinstance(n, int) or n < BLOCKS - 1:
                    dve.wait_ge(s_logit_hi, n + 1)
                    subtract(logit_lo, all_logits[:, :, bass.ds(NB * n + NB, NB)], logit_hi, s_logit_lo)

            mlp(0)
            with dve.Fori(1, BLOCKS - 1) as n:
                mlp(n)
            mlp(BLOCKS - 1)

        @block.scalar
        def _(act):
            def spread(t):
                act.wait_ge(s_gather, 16 * F * (t + 1))
                wait_past(act, s_xt, Q * t)
                for i in range(ROT):
                    nc.scalar.activation(emb_rot[:, :, F * i:F * (i + 1)].rearrange("p d f -> p f d"),
                                         emb[:, :, :], ACT.Copy).then_inc(s_spread, 1)

            def stack_copy(n, made):
                act.wait_ge(s_xt, n + 1)
                wait_past(act, s_prod, made)
                wait_past(act, s_store, 32 * n)
                nc.scalar.activation(x0stack[:, :], ps_x[0:ROWS0, :], ACT.Copy).then_inc(s_stack, 1)

            def relu_maps(z, layer, rows, maps, contracted, done):
                act.wait_ge(s_used, contracted)
                for half in (0, HALF):
                    nc.scalar.activation(maps[half:half + HALF, :], z[rows:rows + HALF, :], ACT.Relu,
                                         bias=cb_sb[rows:rows + HALF, layer:layer + 1]).then_inc(done, 1)

            def relu_direct(z, layer, rows, parity, done):
                nc.scalar.activation(direct[rows:rows + HALF, parity, 0, :], z[rows:rows + HALF, :], ACT.Relu,
                                     bias=cb_sb[rows:rows + HALF, layer:layer + 1]).then_inc(done, 1)

            def relu2(c, parity, contracted):
                act.wait_ge(s_used, contracted)
                nc.scalar.activation(direct[:, parity, 1, :], ps_z2[:, :], ACT.Relu,
                                     bias=cb_sb[:, 2:3]).then_inc(s_direct2, 1)

            def round_hi(c, q, k):
                act.wait_ge(s_prod, upto(c, k))
                wait_split_free(act, c, k, HIS)
                nc.scalar.activation(hi[:, split_slot(q, c, k, HIS), :, :], prod[:, prod_slot(c, k), :, :],
                                     ACT.Copy).then_inc(s_hi, 1)

            def step(t, q):
                c = Q * t + q
                items = items_of(c)
                more, first = items is not LAST_ITEMS, items is FIRST_ITEMS
                ahead = more and items_of(c + 1) is not LAST_ITEMS
                head = at(c, 2, 0)
                for k, (layer, j, kind) in enumerate(items):
                    if k == head:
                        if not first:
                            act.wait_ge(s_prod, upto(c, at(c, 2, I1 - 1)))
                        relu_maps(ps_z1, 1, HALF, maps2, upto(c, I1 - 1), s_maps2)
                    if kind != WHOLE:
                        round_hi(c, q, k)
                    if k == SPREAD_PLACE and q == 2 and ahead:
                        spread(t + 1)
                    if k == place(items, STACK_PLACE) and ahead:
                        stack_copy(c + 2, upto(c, at(c, 0, I0 - 1)))
                    if k == head + DIRECT1_PLACE:
                        relu_direct(ps_z1, 1, 0, q % 2, s_direct1)
                    if k == head + RELU2_PLACE and not first:
                        relu2(c - 1, (q + 1) % 2, upto(c, at(c, 2, I1 - 1)))
                    if k == head + MAPS1_PLACE and more:
                        relu_maps(ps_z0, 0, 0, maps1, upto(c, at(c, 0, I0 - 1)), s_maps1)
                    if k == head + DIRECT0_PLACE and more:
                        wait_past(act, s_sum, c)
                        relu_direct(ps_z0, 0, HALF, (q + 1) % 2, s_direct0)

            act.wait_ge(s_cin_w, 16 * CIN_LOADS)
            nc.scalar.activation(w_hi[:, :, :, :], stage, ACT.Copy).then_inc(s_whi, 1)
            spread(0)
            stack_copy(0, 0)
            relu_maps(ps_z0, 0, 0, maps1, I0, s_maps1)
            relu_direct(ps_z0, 0, HALF, 0, s_direct0)
            stack_copy(1, I0)
            for q in range(Q):
                step(0, q)
            with act.Fori(1, BT - 1) as t:
                for q in range(Q):
                    step(t, q)
            for q in range(Q):
                step(BT - 1, q)
            end = CHUNKS - 1
            act.wait_ge(s_mlp_w, 16 * 4)
            act.wait_ge(s_used, upto(end, I1 - 1))
            nc.scalar.activation(w1_hi, wt1_sb, ACT.Copy).then_inc(s_mlp_hi, 1)
            relu2(end, end % 2, upto(end, len(LAST_ITEMS) - 1))
            nc.scalar.activation(w2_hi, wt2_sb, ACT.Copy).then_inc(s_mlp_hi, 1)

            act.wait_ge(s_mlp_c, 16 * 3)

            def mlp(n):
                for m in range(M1):
                    act.wait_ge(s_h1, M1 * n + m + 1)
                    if m == 0:
                        wait_past(act, s_h2, M2 * n)
                    for h in (hidden, hidden_hi):
                        nc.scalar.activation(h[:, m, :], ps_h1[m], ACT.Relu,
                                             bias=bt1_sb[:, m:m + 1]).then_inc(s_h1r, 1)
                if not isinstance(n, int) or n < BLOCKS - 1:
                    if isinstance(n, int) and n == BLOCKS - 2:
                        act.wait_ge(s_add, ADDS * BT)
                    nc.scalar.activation(logit_hi, all_logits[:, :, bass.ds(NB * n + NB, NB)],
                                         ACT.Copy).then_inc(s_logit_hi, 1)
                for m, z in enumerate((ps_z0, ps_z1)):
                    act.wait_ge(s_h2, M2 * n + m + 1)
                    if m == 0:
                        wait_past(act, s_y, n)
                    nc.scalar.activation(hidden[:, M1 + m, :], z[:, :], ACT.Relu,
                                         bias=bt2_sb[:, m:m + 1]).then_inc(s_h2r, 1)
                act.wait_ge(s_y, n + 1)
                if isinstance(n, int) and n == 0:
                    act.wait_ge(s_sum, CHUNKS)
                nc.scalar.activation(y_sb[0:1, bass.ds(NB * n, NB)], ps_z2[0:1, :], ACT.Copy).then_inc(s_yc, 1)

            mlp(0)
            with act.Fori(1, BLOCKS - 2) as n:
                mlp(n)
            mlp(BLOCKS - 2)
            mlp(BLOCKS - 1)

        @block.tensor
        def _(pe):
            def transposes(n, q):
                wait_past(pe, s_stack, n)
                for d in range(LANES):
                    last = nc.tensor.transpose(ps_x[0:ROWS0, P * d:P * (d + 1)],
                                               emb_rot[:, LANES * q + d, :], ident_sb[:, :])
                last.then_inc(s_xt, 1)

            def whole(item, slot, w, tiles, z, first, final, rows=P):
                pe.wait_ge(s_prod, item)
                for i, tile in enumerate(tiles):
                    last = nc.tensor.matmul(z[:, :], w[0:rows, tile, :], prod[0:rows, slot, i, :],
                                            start=first and i == 0, stop=final and i == len(tiles) - 1)
                last.then_inc(s_used, 1)

            def contract(c, q, k):
                layer, j, kind = items_of(c)[k]
                slot = prod_slot(c, k)
                z = (ps_z0, ps_z1, ps_z2)[layer]
                if j == 0:
                    wait_past(pe, (s_direct0, s_direct1, s_direct2)[layer], c + 1 if layer == 0 else c)
                if layer == 0:
                    whole(upto(c, k), slot, w0_sb, TILES0[j], z, j == 0, j == I0 - 1, ROWS0)
                    return
                if kind == WHOLE:
                    w, wholes = (w1_sb, WHOLE1) if layer == 1 else (w2_sb, WHOLE2)
                    tile = 2 * wholes.index(j)
                    whole(upto(c, k), slot, w, (tile, tile + 1), z, j == 0, j == I1 - 1)
                    return
                hi_slot, lo_slot = split_slot(q, c, k, HIS), split_slot(q, c, k, LOS)
                row = SPLIT1.index(j) if layer == 1 else len(SPLIT1) + SPLIT2.index(j)
                pe.wait_ge(s_hi, upto(c, k, (V, G)))
                for i in range(2):
                    for w in (w_lo, w_hi):
                        nc.tensor.matmul(z[:, :], w[:, row, i, :], hi[:, hi_slot, i, :],
                                         start=j == 0 and i == 0 and w is w_lo, stop=False)
                wait_lo(pe, c, k)
                for i in range(2):
                    last = nc.tensor.matmul(z[:, :], w_hi[:, row, i, :], lo[:, lo_slot, i, :],
                                            start=False, stop=j == I1 - 1 and i == 1)
                last.then_inc(s_used, 1)

            def step(t, q):
                c = Q * t + q
                items = items_of(c)
                ahead = items is not LAST_ITEMS and items_of(c + 1) is not LAST_ITEMS
                for k in range(len(items)):
                    if k == place(items, TRANSPOSE_PLACE) and ahead:
                        if q == Q - 2:
                            pe.wait_ge(s_spread, ROT * (t + 2))
                        transposes(c + 2, (q + 2) % Q)
                    contract(c, q, k)

            pe.wait_ge(s_cin_w, 16 * CIN_LOADS)
            pe.wait_ge(s_spread, ROT)
            for q in range(2):
                transposes(q, q)
            pe.wait_ge(s_w0, 1)
            for k in range(I0):
                contract(-1, 0, k)
            pe.wait_ge(s_wlo, 1)
            for q in range(Q):
                step(0, q)
            with pe.Fori(1, BT - 1) as t:
                for q in range(Q):
                    step(t, q)
            for q in range(Q):
                step(BT - 1, q)

            pe.wait_ge(s_mlp_c, 16 * 3)
            pe.wait_ge(s_mlp_w, 16 * 4)
            pe.wait_ge(s_reload, 16)
            pe.wait_ge(s_direct0, CHUNKS)
            pe.wait_ge(s_direct1, CHUNKS)

            def three_passes(z, w_high, w_low, x_high, x_low, first, final):
                nc.tensor.matmul(z, w_low, x_high, start=first, stop=False)
                nc.tensor.matmul(z, w_high, x_high, start=False, stop=False)
                return nc.tensor.matmul(z, w_high, x_low, start=False, stop=final)

            def mlp(n):
                cols = bass.ds(NB * n, NB)
                wait_past(pe, s_h1r, 2 * M1 * n)
                start = isinstance(n, int) and n == 0
                if not start:
                    pe.wait_ge(s_logit_lo, n)
                for m in range(M1):
                    ms = slice(P * m, P * (m + 1))
                    for k in range(2):
                        if start:
                            nc.tensor.matmul(ps_h1[m], wt1_sb[:, k, ms], all_logits[:, k, cols], start=k == 0,
                                             stop=False)
                        else:
                            three_passes(ps_h1[m], w1_hi[:, k, ms], w1_lo[:, k, ms], logit_hi[:, k, :],
                                         logit_lo[:, k, :], k == 0, False)
                    nc.tensor.matmul(ps_h1[m], wt1d_sb[:, ms], dense_sb[:, cols], start=False, stop=True) \
                        .then_inc(s_h1, 1)
                wait_past(pe, s_h2r, M2 * n)
                if start:
                    pe.wait_ge(s_mlp_lo, 2)
                for k in range(M1):
                    pe.wait_ge(s_h1_lo, M1 * n + k + 1)
                    for m, z in enumerate((ps_z0, ps_z1)):
                        ms = slice(P * m, P * (m + 1))
                        last = three_passes(z[:, :], w2_hi[:, k, ms], w2_lo[:, k, ms], hidden_hi[:, k, :],
                                            hidden_lo[:, k, :], k == 0, k == M1 - 1)
                        if k == M1 - 1:
                            last.then_inc(s_h2, 1)
                wait_past(pe, s_yc, n)
                if isinstance(n, int) and n == 0:
                    pe.wait_ge(s_direct2, CHUNKS)
                for k in range(M2):
                    pe.wait_ge(s_h2r, M2 * n + k + 1)
                    last = nc.tensor.matmul(ps_z2[0:1, :], wt3_sb[:, k:k + 1], hidden[:, M1 + k, :],
                                            start=k == 0, stop=k == M2 - 1)
                last.then_inc(s_y, 1)

            mlp(0)
            with pe.Fori(1, BLOCKS) as n:
                mlp(n)


def kernel(**inputs):
    import numpy as np
    import concourse.bacc as bacc
    from concourse.bass_utils import run_bass_kernel_spmd as run

    f32 = np.float32
    x = {k: np.asarray(v) for k, v in inputs.items()}

    w0 = x["L0_rec_w0"]
    w0a, w0b = np.zeros((P, T0, S), f32), np.zeros((P, T0, S), f32)
    h = np.arange(F)
    for n, r in enumerate(ROTATIONS):
        t, i = divmod(n, ROT)
        k = (h + r) % F
        w0a[i * F + h, t] = w0[h, k]
        if r:
            w0b[i * F + h, t] = w0[k, h]

    def pairs(w):
        full = np.zeros((2 * T1, HALF, S), f32)
        full[:F] = w
        return np.ascontiguousarray(full.reshape(T1, P, S).transpose(1, 0, 2))

    swap = np.r_[HALF:S, 0:HALF]
    w1, w2 = pairs(x["L0_rec_w1"][:, :, swap]), pairs(x["L0_rec_w2"])

    def tiles(w, items):
        return np.ascontiguousarray(w[:, [2 * j + i for j in items for i in range(2)]])

    cin_bias = np.stack([x["L0_rec_b0"], x["L0_rec_b1"][swap], x["L0_rec_b2"]], axis=1)
    wt1 = x["W_top1"][np.r_[swap, S:S + S + DENSE]]
    arrays = {
        "ids": np.ascontiguousarray(x["ids"].reshape(BT, P, F)),
        "dense_t": np.ascontiguousarray(x["dense_ctx"].T),
        "ident": np.eye(P, dtype=f32),
        "w0a": w0a,
        "w0b": w0b,
        "w1_whole": tiles(w1, WHOLE1),
        "w2_whole": tiles(w2, WHOLE2),
        "w_split": np.concatenate([tiles(w1, SPLIT1), tiles(w2, SPLIT2)], axis=1),
        "cin_bias": np.ascontiguousarray(cin_bias),
        "wt1": np.ascontiguousarray(wt1),
        "bt1": np.ascontiguousarray(x["b_top1"].reshape(M1, P).T),
        "wt2": x["W_top2"],
        "bt2": np.ascontiguousarray(x["b_top2"].reshape(M2, P).T),
        "wt3": np.ascontiguousarray(x["W_top3"].reshape(M2, P).T),
    }
    tables = {f"tbl_{f}": x[f"tbl_{f}"] for f in range(F)}

    nc = bacc.Bacc("TRN2", target_bir_lowering=False, num_devices=1)

    def dram(name, a):
        return nc.dram_tensor(name, a.shape, mybir.dt.from_np(a.dtype), kind="ExternalInput").ap()

    tbl_aps = [dram(f"tbl_{f}", tables[f"tbl_{f}"]) for f in range(F)]
    aps = {name: dram(name, a) for name, a in arrays.items()}
    out = nc.dram_tensor("out", (B, 1), F32, kind="ExternalOutput").ap()
    x0rows = nc.dram_tensor("x0rows", (2, ROWS, CHUNK), F32, kind="Internal").ap()
    logits = nc.dram_tensor("logits", (P, 2, P * (BT - 1)), F32, kind="Internal").ap()
    dlrm_tower(nc, tbl_aps, x0rows=x0rows, logits=logits, out=out, **aps)
    arrays.update(tables)
    r = run(nc, [arrays], core_ids=[0])
    return r.results[0]["out"]
```
